# Optimizing a Trainium2 kernel written in Bass

```python
import numpy as np
import jax
import jax.numpy as jnp

def _softmax(x, axis=-1):
    return jax.nn.softmax(x, axis=axis)

def _gelu(x):
    return jax.nn.gelu(x, approximate=True)

def _silu(x):
    return jax.nn.silu(x)

def _sigmoid(x):
    return jax.nn.sigmoid(x)

def _layernorm(x, axis=-1, eps=1e-05):
    m = jnp.mean(x, axis=axis, keepdims=True)
    v = jnp.var(x, axis=axis, keepdims=True)
    return (x - m) / jnp.sqrt(v + eps)

def _scatter_add(tgt, idx, src, axis=0):
    return tgt.at[idx].add(src)

def _segment_sum(src, seg, n):
    return jax.ops.segment_sum(src, seg, n)
kernel_name = 'mk_flamingo_gated_d1_seqx_r8_e6acc1'

def setup_inputs(seed: int=0):
    np.random.seed(seed)
    _w = jnp.asarray

    def _rec_inputs():
        import jax
        import jax.numpy as jnp
        _rk = jax.random.key(seed)
        x = -0.000125 + 0.9999 * jax.random.normal(jax.random.fold_in(_rk, 1), (16, 56, 128), jnp.float32)
        _lenS = 56 - jax.random.randint(jax.random.fold_in(_rk, 7), (16,), 0, max(1, 56 // 4) + 1, jnp.int32)
        _lenS2 = 1500 - jax.random.randint(jax.random.fold_in(_rk, 8), (16,), 0, max(1, 1500 // 4) + 1, jnp.int32)
        _ctx_1024P = jax.random.normal(jax.random.fold_in(_rk, 11), (16, 16, 128), jnp.float32)
        _ctx_1024c = jax.random.dirichlet(jax.random.fold_in(_rk, 511), 0.3 * jnp.ones((16,), jnp.float32), (16, 1500))
        _ctx_1024t = jnp.einsum('bsk,bkd->bsd', _ctx_1024c, _ctx_1024P)
        _ctx_1024t = _ctx_1024t * jax.lax.rsqrt(jnp.mean(jnp.square(_ctx_1024t)) + 1e-12) * 0.953939
        ctx_1024 = -0.000514642 + 1.00011 * (_ctx_1024t + 0.3 * jax.random.normal(jax.random.fold_in(_rk, 611), (16, 1500, 128), jnp.float32))
        _validS = jnp.arange(56)[None, :] < _lenS[:, None]
        _validS2 = jnp.arange(1500)[None, :] < _lenS2[:, None]
        _causal = jnp.tril(jnp.ones((56, 56), dtype=bool))
        mask_BxS2_bf1 = jnp.ones((16, 1500), dtype=bool)
        _g = jax.random.normal(jax.random.fold_in(_rk, 9001), (2, 1), jnp.float32)
        _g = jnp.sign(_g) * jnp.maximum(jnp.abs(_g), 1.0) + (_g == 0) * 1.0
        g_xattn = _g[0]
        g_ffn = _g[1]
        return (x, ctx_1024, mask_BxS2_bf1, g_xattn, g_ffn)
    x, ctx_1024, mask_BxS2_bf1, g_xattn, g_ffn = _rec_inputs()

    def _L0_xattn_setup():
        import jax, jax.numpy as jnp
        import numpy as np
        EPS = 1e-06
        NUM_HEADS = 16
        DIM_HEADS = 64

        def _ln(x, scale, bias):
            mu = jnp.mean(x, axis=-1, keepdims=True)
            var = jnp.mean(jnp.square(x - mu), axis=-1, keepdims=True)
            return (x - mu) * jax.lax.rsqrt(var + EPS) * scale + bias
        key = jax.random.key(seed)
        ks = jax.random.split(key, 8)
        b, n, m, dim, ctx_dim = (8, 512, 32, 128, 128)
        inner = NUM_HEADS * DIM_HEADS
        x = jax.random.normal(ks[0], (b, n, dim), dtype=jnp.float32)
        context = jax.random.normal(ks[1], (b, m, ctx_dim), dtype=jnp.float32)
        mask = jnp.ones((b, m), dtype=bool)
        Wq = jax.random.normal(ks[2], (dim, inner), dtype=jnp.float32) / np.sqrt(dim)
        Wkv = jax.random.normal(ks[3], (ctx_dim, 2 * inner), dtype=jnp.float32) / np.sqrt(ctx_dim)
        null_kv = jax.random.normal(ks[4], (2, DIM_HEADS), dtype=jnp.float32)
        Wo = jax.random.normal(ks[5], (inner, dim), dtype=jnp.float32) / np.sqrt(inner)
        return {'x': x, 'context': context, 'mask': mask, 'ln1_s': jnp.ones((dim,), jnp.float32), 'ln1_b': jnp.zeros((dim,), jnp.float32), 'lnc_s': jnp.ones((ctx_dim,), jnp.float32), 'lnc_b': jnp.zeros((ctx_dim,), jnp.float32), 'Wq': Wq, 'Wkv': Wkv, 'null_kv': null_kv, 'Wo': Wo, 'lno_s': jnp.ones((dim,), jnp.float32), 'lno_b': jnp.zeros((dim,), jnp.float32)}
    _L0_xattn_all = _L0_xattn_setup()
    _L0_xattn_in = {k: v for k, v in _L0_xattn_all.items() if k in ('ln1_s', 'ln1_b', 'lnc_s', 'lnc_b', 'Wq', 'Wkv', 'null_kv', 'Wo', 'lno_s', 'lno_b')}
    del _L0_xattn_all

    def _L0_ffn_setup():
        import jax, jax.numpy as jnp
        import numpy as np
        B, S, H, F, E = (4, 256, 128, 512, 8)
        key = jax.random.key(seed)
        ks = jax.random.split(key, 8)
        s = 1.0 / np.sqrt(H)
        sf = 1.0 / np.sqrt(F)
        return {'x': jax.random.normal(ks[0], (B, S, H), jnp.float32), 'wr': jax.random.uniform(ks[1], (H, E), jnp.float32, -s, s), 'br': jax.random.uniform(ks[2], (E,), jnp.float32, -s, s), 'w1': jax.random.uniform(ks[3], (E, H, F), jnp.float32, -s, s), 'b1': jax.random.uniform(ks[4], (E, F), jnp.float32, -s, s), 'w2': jax.random.uniform(ks[5], (E, F, H), jnp.float32, -sf, sf), 'b2': jax.random.uniform(ks[6], (E, H), jnp.float32, -sf, sf)}
    _L0_ffn_all = _L0_ffn_setup()
    _L0_ffn_in = {k: v for k, v in _L0_ffn_all.items() if k in ('wr', 'br', 'w1', 'b1', 'w2', 'b2')}
    del _L0_ffn_all
    return {'x': x, 'ctx_1024': ctx_1024, 'mask_BxS2_bf1': mask_BxS2_bf1, 'g_xattn': g_xattn, 'g_ffn': g_ffn, 'L0_xattn_ln1_s': _L0_xattn_in['ln1_s'], 'L0_xattn_ln1_b': _L0_xattn_in['ln1_b'], 'L0_xattn_lnc_s': _L0_xattn_in['lnc_s'], 'L0_xattn_lnc_b': _L0_xattn_in['lnc_b'], 'L0_xattn_Wq': _L0_xattn_in['Wq'], 'L0_xattn_Wkv': _L0_xattn_in['Wkv'], 'L0_xattn_null_kv': _L0_xattn_in['null_kv'], 'L0_xattn_Wo': _L0_xattn_in['Wo'], 'L0_xattn_lno_s': _L0_xattn_in['lno_s'], 'L0_xattn_lno_b': _L0_xattn_in['lno_b'], 'L0_ffn_wr': _L0_ffn_in['wr'], 'L0_ffn_br': _L0_ffn_in['br'], 'L0_ffn_w1': _L0_ffn_in['w1'], 'L0_ffn_b1': _L0_ffn_in['b1'], 'L0_ffn_w2': _L0_ffn_in['w2'], 'L0_ffn_b2': _L0_ffn_in['b2']}

def reference(x, ctx_1024, mask_BxS2_bf1, g_xattn, g_ffn, L0_xattn_ln1_s, L0_xattn_ln1_b, L0_xattn_lnc_s, L0_xattn_lnc_b, L0_xattn_Wq, L0_xattn_Wkv, L0_xattn_null_kv, L0_xattn_Wo, L0_xattn_lno_s, L0_xattn_lno_b, L0_ffn_wr, L0_ffn_br, L0_ffn_w1, L0_ffn_b1, L0_ffn_w2, L0_ffn_b2):
    import jax
    import jax.numpy as jnp

    def _L0_xattn_ref(x, context, mask, ln1_s, ln1_b, lnc_s, lnc_b, Wq, Wkv, null_kv, Wo, lno_s, lno_b):
        import jax, jax.numpy as jnp
        import numpy as np
        EPS = 1e-06
        NUM_HEADS = 16
        DIM_HEADS = 64

        def _ln(x, scale, bias):
            mu = jnp.mean(x, axis=-1, keepdims=True)
            var = jnp.mean(jnp.square(x - mu), axis=-1, keepdims=True)
            return (x - mu) * jax.lax.rsqrt(var + EPS) * scale + bias
        b, n, _ = x.shape
        h, d = (NUM_HEADS, DIM_HEADS)
        scale = h ** (-0.5)
        xn = _ln(x, ln1_s, ln1_b)
        cn = _ln(context, lnc_s, lnc_b)
        q = xn @ Wq
        kv = cn @ Wkv
        k, v = jnp.split(kv, 2, axis=-1)

        def to_heads(t):
            return t.reshape(t.shape[0], t.shape[1], h, d).transpose(0, 2, 1, 3)
        q, k, v = (to_heads(q), to_heads(k), to_heads(v))
        nk = jnp.broadcast_to(null_kv[0], (b, h, 1, d))
        nv = jnp.broadcast_to(null_kv[1], (b, h, 1, d))
        k = jnp.concatenate((nk, k), axis=2)
        v = jnp.concatenate((nv, v), axis=2)
        sim = jnp.einsum('bhid,bhjd->bhij', q * scale, k)
        mfull = jnp.pad(mask, ((0, 0), (1, 0)), constant_values=True)[:, None, None, :]
        max_neg = -jnp.finfo(sim.dtype).max
        sim = jnp.where(mfull, sim, max_neg)
        attn = jax.nn.softmax(sim, axis=-1)
        out = jnp.einsum('bhij,bhjd->bhid', attn, v)
        out = out.transpose(0, 2, 1, 3).reshape(b, n, h * d)
        out = out @ Wo
        return _ln(out, lno_s, lno_b)

    def _L0_ffn_ref(x, wr, br, w1, b1, w2, b2):
        import jax, jax.numpy as jnp
        import numpy as np
        B, S, H, F, E = (4, 256, 128, 512, 8)
        scores = jnp.einsum('bsh,he->bse', x, wr) + br
        expert_id = jnp.argmax(scores, axis=-1)
        h = jnp.einsum('bsh,ehf->ebsf', x, w1) + b1[:, None, None, :]
        h = jax.nn.gelu(h, approximate=False)
        y = jnp.einsum('ebsf,efh->ebsh', h, w2) + b2[:, None, None, :]
        one_hot = jax.nn.one_hot(expert_id, E, dtype=x.dtype)
        out = jnp.einsum('ebsh,bse->bsh', y, one_hot)
        return out
    x = x + jnp.tanh(g_xattn[0]) * _L0_xattn_ref(_layernorm(x, axis=-1), ctx_1024, mask_BxS2_bf1, L0_xattn_ln1_s, L0_xattn_ln1_b, L0_xattn_lnc_s, L0_xattn_lnc_b, L0_xattn_Wq, L0_xattn_Wkv, L0_xattn_null_kv, L0_xattn_Wo, L0_xattn_lno_s, L0_xattn_lno_b)
    x = x + jnp.tanh(g_ffn[0]) * _L0_ffn_ref(_layernorm(x, axis=-1), L0_ffn_wr, L0_ffn_br, L0_ffn_w1, L0_ffn_b1, L0_ffn_w2, L0_ffn_b2)
    return x

_drawn_inputs = setup_inputs


def setup_inputs(seed=0):
    import zlib

    import numpy as np

    out = dict(_drawn_inputs(seed))
    spreads = {'L0_xattn_ln1_s': (1.0, 0.2),
     'L0_xattn_ln1_b': (0.0, 0.1),
     'L0_xattn_lnc_s': (1.0, 0.2),
     'L0_xattn_lnc_b': (0.0, 0.1),
     'L0_xattn_lno_s': (1.0, 0.2),
     'L0_xattn_lno_b': (0.0, 0.1)}
    factors = {'L0_xattn_null_kv': 3.369, 'L0_ffn_b1': 4.16, 'L0_ffn_b2': 2.95}
    for name, (base, spread) in spreads.items():
        noise = np.random.default_rng([zlib.crc32(name.encode()), seed]).standard_normal(out[name].shape)
        drawn = base * np.exp(spread * noise) if base else spread * noise
        out[name] = jnp.asarray(drawn.astype(out[name].dtype))
    for name, factor in factors.items():
        out[name] = (out[name] * factor).astype(out[name].dtype)
    return out
```

```python
import concourse.bass as bass
from concourse import mybir
from contextlib import ExitStack


def gated_cross_attention_moe_kernel(nc, x, ctx, mask, g_xattn, g_ffn, ln1_s, ln1_b, lnc_s, lnc_b,
                                     Wq, Wkv, null_kv, Wo, lno_s, lno_b, wr, br, w1, b1, w2, b2,
                                     ident_f32, ident_f16, out):
    fp32, fp16 = mybir.dt.float32, mybir.dt.float16
    ALU = mybir.AluOpType
    ACT = mybir.ActivationFunctionType
    AX = mybir.AxisListType.X

    B, NQ, D = x.shape
    NKEY = ctx.shape[1]
    INNER = Wq.shape[1]
    DH = null_kv.shape[1]
    H = INNER // DH
    NP = H // 2
    E, _, F = w1.shape
    FC = F // 128
    NC = 12
    CK = NKEY // NC
    R = H * NQ
    HR = R // 2
    RT = R // 128
    KB = NKEY // 3
    NMX = 3 * RT
    TT = 2 * NQ
    NT = B // 2
    NTOK = B * NQ
    HC = NC // 2
    PB = 4
    ATT_SCALE = float(H) ** -0.5
    W_SCALE = 64.0
    SHIFT = 10 * 0.6931471805599453
    MASKED = 60000.0
    MASK_BIAS = 1.0e37
    TP = CK + 1

    ctx_v = ctx.rearrange("b (p c) d -> b p c d", c=NC)
    x_v = x.rearrange("(t u) n d -> (u n) t d", u=2)
    out_v = out.rearrange("(t u) n d -> (u n) t d", u=2)
    r_dram = nc.dram_tensor("r_scratch", (2, R), fp32, kind="Internal").ap()

    es = ExitStack()
    with es:
        def sb(name, shape, dt=fp32):
            return es.enter_context(nc.sbuf_tensor(name, shape, dt))

        def sem(name):
            return es.enter_context(nc.semaphore(name))

        raw = sb("raw", [CK, 2, NC, D])
        zf = sb("zf", [CK, NC, D])
        zh = sb("zh", [CK, 2, NC, D], fp16)
        zl = sb("zl", [CK, 2, NC, D], fp16)
        zTh = sb("zTh", [D, 2, NKEY], fp16)
        zTl = sb("zTl", [D, 2, NKEY], fp16)
        qh = sb("qh", [D, 2, R], fp16)
        ql = sb("ql", [D, 2, R], fp16)
        PP = sb("PP", [128, 2, PB, R], fp16)
        Ph, Pl = PP[0:CK, 0], PP[0:CK, 1]
        mask_s = sb("mask_s", [CK, B, NC], mybir.dt.uint8)
        maskf = sb("maskf", [CK, B, NC])
        mbias = sb("mbias", [CK, B, NC])
        mcol = sb("mcol", [CK, B, NC], fp16)
        mb = sb("mb", [CK, 2, NC])
        Af = sb("Af", [D, R])
        Rb = sb("Rb", [D, R])
        An = sb("An", [D, H, 2, NQ])
        G = sb("G", [D, H, D])
        M = sb("M", [D, H, D])
        st = sb("st", [CK, NC, 6])
        mu = sb("mu", [CK, NC])
        rs = sb("rs", [CK, NC])
        tmp1 = sb("tmp1", [CK, NC])
        tmp2 = sb("tmp2", [CK, NC])
        mhalf = sb("mhalf", [128, NC])
        nullrow = sb("nullrow", [1, R])
        null7 = sb("null7", [128, RT])
        mx3 = sb("mx3", [128, RT, 3])
        negm = sb("negm", [128, RT])
        mneg = sb("mneg", [128, RT], fp16)
        t7 = sb("t7", [128, RT])
        P07 = sb("P07", [128, 2, RT])
        S7 = sb("S7", [128, RT])
        tot7 = sb("tot7", [128, RT])
        R7 = sb("R7", [128, RT])
        idf = sb("idf", [128, 128])
        idh = sb("idh", [128, 128], fp16)
        T = sb("T", [D, D])
        rowmask = sb("rowmask", [D, 1])
        rowbias = sb("rowbias", [D, 1])
        cs = sb("cs", [D, 2])
        l1 = sb("l1", [D, 2])
        nkv = sb("nkv", [128, 2])
        nvrep = sb("nvrep", [128, TT])
        NVb = sb("NVb", [TT, D])
        gh = sb("gh", [128, 2, FC, NTOK], fp16)
        gl = PP
        early = gh[:, :, :, :].rearrange("p a f n -> p (a f n)").bitcast(fp32)
        Wq_s = early[:, 0:INNER]
        Wkv_s = early[:, INNER:3 * INNER]
        Wo_s = sb("Wo_s", [128, NP, D])
        WqT = sb("WqT", [128, NP, D])
        WkT = sb("WkT", [128, NP, D])
        WvT = sb("WvT", [128, NP, D])
        x_s = sb("x_s", [TT, NT, D])
        y_s = sb("y_s", [TT, NT, D])
        xn = sb("xn", [TT, NT, D])
        st8 = sb("st8", [TT, NT, 6])
        mu8 = sb("mu8", [TT, NT])
        rs8 = sb("rs8", [TT, NT])
        t81 = sb("t81", [TT, NT])
        t82 = sb("t82", [TT, NT])
        xT = sb("xT", [D, NTOK])
        xTh = sb("xTh", [D, NTOK], fp16)
        xTl = sb("xTl", [D, NTOK], fp16)
        lno_r = sb("lno_r", [TT, 2, D])
        gates = sb("gates", [TT, 2])
        wr_s = sb("wr_s", [D, E])
        br_r = sb("br_r", [TT, E])
        b1_s = sb("b1_s", [E * FC, 128])
        b1T = sb("b1T", [128, E * FC])
        b2_s = sb("b2_s", [E, D])
        sc = sb("sc", [TT, NT, E])
        scm = sb("scm", [TT, NT])
        eqm = sb("eqm", [TT, NT, E])
        erow = sb("erow", [TT, E])
        esel = sb("esel", [TT, NT])
        oneh = sb("oneh", [TT, NT, E])
        onehs = sb("onehs", [TT, NT, E])
        onehT = sb("onehT", [E, NT, TT])
        wst = sb("wst", [D, 2, 2, F])
        wh = sb("wh", [128, E, 2, F], fp16)
        wl = sb("wl", [128, E, 2, F], fp16)
        moe = sb("moe", [TT, NT, D])

        S = es.enter_context(nc.psum_tensor("S", [128, 4, 512], fp32))
        A = es.enter_context(nc.psum_tensor("A", [128, 2, 512], fp32))
        X = es.enter_context(nc.psum_tensor("X", [128, 2, 512], fp32))
        Xh = X[:, :, :].bitcast(fp16)
        XT = [Xh[:, i, 0:HC * TP].rearrange("p (c k) -> p c k", k=TP) for i in range(2)]

        ld_w = sem("ld_w")
        ld_x = sem("ld_x")
        ld_m = sem("ld_m")
        mask_ready = sem("mask_ready")
        ld_ctx = [sem("ld_ctx_even"), sem("ld_ctx_odd")]
        ld_f = sem("ld_f")
        ld_we = [sem("ld_we_even"), sem("ld_we_odd")]
        s7_in = sem("s7_in")
        null_in = sem("null_in")
        r_out = sem("r_out")
        rb_in = sem("rb_in")
        out_done = sem("out_done")
        dve_step = sem("dve_step")
        pool_step = sem("pool_step")
        pool_gate = sem("pool_gate")
        sp_gate = sem("sp_gate")
        const_ready = sem("const_ready")
        t_ready = sem("t_ready")
        wt_ready = sem("wt_ready")
        wt_copied = sem("wt_copied")
        fold_ready = sem("fold_ready")
        gm_ready = sem("gm_ready")
        gm_copied = sem("gm_copied")
        nv_ready = sem("nv_ready")
        x8_stats = sem("x8_stats")
        x8_small = sem("x8_small")
        xt_in = sem("xt_in")
        xt_ready = sem("xt_ready")
        xt_copied = sem("xt_copied")
        sim_done = sem("sim_done")
        hi_done = sem("hi_done")
        e_done = sem("e_done")
        lo_done = sem("lo_done")
        pv_done = sem("pv_done")
        a_copied = sem("a_copied")
        zt_ready = sem("zt_ready")
        zt_copied = sem("zt_copied")
        q_ready = sem("q_ready")
        qhi_done = sem("qhi_done")
        qlo_done = sem("qlo_done")
        null_done = sem("null_done")
        mx_ready = sem("mx_ready")
        mx_red = sem("mx_red")
        mneg_done = sem("mneg_done")
        t7_done = sem("t7_done")
        p0_done = sem("p0_done")
        mt_ready = sem("mt_ready")
        slot_done = sem("slot_done")
        stats_done = sem("stats_done")
        zc_done = sem("zc_done")
        mb_done = sem("mb_done")
        split1_done = sem("split1_done")
        split2_done = sem("split2_done")
        r_done = sem("r_done")
        an_done = sem("an_done")
        y_ready = sem("y_ready")
        y_done = sem("y_done")
        wsplit = sem("wsplit")
        tanh_done = sem("tanh_done")
        b1_ready = sem("b1_ready")
        b1_copied = sem("b1_copied")
        sc_ready = sem("sc_ready")
        xhl_done = sem("xhl_done")
        oneh_done = sem("oneh_done")
        ohT_ready = sem("ohT_ready")
        ohT_copied = sem("ohT_copied")
        acc0_ready = sem("acc0_ready")
        acc0_copied = sem("acc0_copied")
        h_ready = sem("h_ready")
        gh_done = sem("gh_done")
        gf_done = sem("gf_done")
        gl_done = sem("gl_done")
        ye_ready = sem("ye_ready")
        ye_done = sem("ye_done")
        fin_done = sem("fin_done")

        class Chain:

            def __init__(self, s, wait_ge):
                self.sem, self.wait_ge, self.base, self.n = s, wait_ge, 0, 0

            def wait(self):
                self.wait_ge(self.sem, self.base + self.n)

            def link(self, ins):
                ins.then_inc(self.sem, 1)
                self.n += 1
                self.wait()

        def waiter(eng, gate):
            def wait_ge(s, value):
                eng.wait_ge(s, value)
                if not isinstance(value, int):
                    eng.sem_inc(gate, 1)
            return wait_ge

        def ahead(b, c):
            return (b, c + 2) if c + 2 < NC else (b + 1, c + 2 - NC)

        def flags(b):
            return dict(main=b >= 0, prep=b + 1 < B, znext=b + 2 < B, load=b + 3 < B,
                        tail=b >= 1, b_ge2=b >= 2, y=b >= 2 and b % 2 == 0, t0y=b >= 3 and b % 2 == 1,
                        prev=b >= 0, wexp=None)

        STEADY = [flags(4), flags(5)]
        for f_ in STEADY:
            f_["load"] = True

        def iterate(eng, body, last):
            for b in (-1, 0, 1):
                body(b, b % 2, flags(b))
            with eng.Fori(2, last - 1, 2) as i:
                body(i, 0, STEADY[0])
                body(i + 1, 1, STEADY[1])
            for b in range(last, B):
                body(b, b % 2, flags(b))

        block = es.enter_context(nc.Block())

        @block.sync
        def _(sp):
            sp.dma_start(x_s[:, :, :], x_v).then_inc(ld_x, 16)
            sp.dma_start(raw[:, 0], ctx_v[0]).then_inc(ld_ctx[0], 16)
            with nc.allow_non_contiguous_dma("the mask's 12-byte runs"):
                sp.dma_start(mask_s[:, :, :], mask.rearrange("b (p c) -> p b c", c=NC)).then_inc(ld_m, 16)
            sp.dma_start(raw[:, 1], ctx_v[1]).then_inc(ld_ctx[1], 16)

            wait_ge = waiter(sp, sp_gate)

            def move_null(n):
                wait_ge(null_done, 2 * n + 2)
                sp.dma_start(null7[:, :], nullrow[0:1, :].rearrange("o (r t) -> o r t", t=RT)).then_inc(null_in, 16)

            def body(b, p, f):
                if f["load"]:
                    wait_ge(zc_done, b + 2)
                    wait_ge(stats_done, b + 2)
                    sp.dma_start(raw[:, 1 - p], ctx_v[b + 3]).then_inc(ld_ctx[1 - p], 16)
                if f["tail"]:
                    wait_ge(a_copied, b)
                    if f["b_ge2"]:
                        wait_ge(r_done, b - 1)
                    sp.dma_start(S7[:, :], Af[0:1, :].rearrange("o (r t) -> o r t", t=RT)).then_inc(s7_in, 16)
                if f["tail"]:
                    wait_ge(r_done, b)
                    sp.dma_start(r_dram[0, :].rearrange("(r t) -> r t", t=RT), R7[:, :]).then_inc(r_out, 16)
                    wait_ge(r_out, 16 * b)
                    if f["b_ge2"]:
                        wait_ge(an_done, b - 1)
                    sp.dma_start(Rb[:, :], r_dram[0:1, :].partition_broadcast(128)).then_inc(rb_in, 16)
                if f["znext"]:
                    wait_ge(t7_done, b + 2)
                    move_null(b + 2)

            move_null(0)
            iterate(sp, body, B - 4)
            b = B
            sp.wait_ge(a_copied, b)
            sp.wait_ge(r_done, b - 1)
            sp.dma_start(S7[:, :], Af[0:1, :].rearrange("o (r t) -> o r t", t=RT)).then_inc(s7_in, 16)
            sp.wait_ge(r_done, b)
            sp.dma_start(r_dram[0, :].rearrange("(r t) -> r t", t=RT), R7[:, :]).then_inc(r_out, 16)
            sp.wait_ge(r_out, 16 * b)
            sp.wait_ge(an_done, b - 1)
            sp.dma_start(Rb[:, :], r_dram[0:1, :].partition_broadcast(128)).then_inc(rb_in, 16)
            sp.wait_ge(fin_done, 1)
            sp.dma_start(out_v, xn[:, :, :]).then_inc(out_done, 16)
            sp.wait_ge(out_done, 16)

        @block.gpsimd
        def _(pool):
            wait_ge = waiter(pool, pool_gate)
            ch = Chain(pool_step, wait_ge)

            def ln_small(s, m, r, t1, t2, eps):
                n = m.shape[1]
                ch.link(pool.tensor_tensor(t1, s[:, :, 1], s[:, :, 4], ALU.add))
                ch.link(pool.tensor_scalar(m, t1, 0.5, 0.0, ALU.mult, ALU.add))
                ch.link(pool.tensor_tensor(t1, s[:, :, 1], s[:, :, 4], ALU.subtract))
                ch.link(pool.tensor_tensor(t2, t1, t1, ALU.mult))
                ch.link(pool.tensor_scalar(t1, t2, D / 4.0, float(D) * eps, ALU.mult, ALU.add))
                ch.link(pool.tensor_tensor(t2, s[:, :, 2], s[:, :, 5], ALU.add))
                ch.link(pool.tensor_tensor(t2, t1, t2, ALU.add))
                ch.link(pool.tensor_scalar(t1, t2, 1.0 / D, 0.0, ALU.mult, ALU.add))
                ch.link(pool.tensor_tensor(r, t1, mhalf[0:m.shape[0], 0:n], ALU.pow))

            def wide(v):
                return v.unsqueeze(2).broadcast_to([CK, NC, D])

            def znorm():
                ln_small(st[:, :, :], mu[:, :], rs[:, :], tmp1[:, :], tmp2[:, :], 1e-6)

            def centre(p):
                ins = pool.tensor_tensor(zf[:, :, :], raw[:, p], wide(mu[:, :]), ALU.subtract)
                ins.then_inc(zc_done, 1)
                return ins

            def scale():
                ch.link(pool.tensor_tensor(zf[:, :, :], zf[:, :, :], wide(rs[:, :]), ALU.mult))

            def split(n, p, c0, done):
                cols = mcol[:, n, c0:c0 + HC] if isinstance(n, int) else \
                    mcol[:, :, :].rearrange("p b c -> p (b c)")[:, bass.ds(n * NC + c0, HC)]
                ch.link(pool.tensor_copy(zh[:, p, c0:c0 + HC, 0], cols))
                hi, lo, z = zh[:, p, c0:c0 + HC, 1:D], zl[:, p, c0:c0 + HC, 1:D], zf[:, c0:c0 + HC, 1:D]
                ch.link(pool.tensor_copy(hi, z))
                pool.tensor_tensor(lo, z, hi, ALU.subtract).then_inc(done, 1)

            def split_expert(e):
                w = wst[:, e % 2]
                pool.wait_ge(ld_we[e % 2], 32 * (e // 2 + 1))
                ch.link(pool.tensor_scalar(w, w, W_SCALE, 0.0, ALU.mult, ALU.add))
                ch.link(pool.tensor_copy(wh[:, e], w))
                pool.tensor_tensor(wl[:, e], w, wh[:, e], ALU.subtract).then_inc(wsplit, 1)

            pool.memset(mhalf[:, :], -0.5)
            pool.memset(zl[:, :, :, 0:1], 0.0)
            for e in range(E):
                pool.memset(erow[:, e:e + 1], float(e - E))
            ch.link(pool.memset(rowmask[:, :], 1.0))
            ch.link(pool.memset(rowmask[0:1, :], 0.0))
            ch.link(pool.memset(rowbias[:, :], 0.0))
            ch.link(pool.memset(rowbias[0:1, :], -1.0))
            pool.memset(T[0:1, :], 0.0).then_inc(const_ready, 1)

            for i, eps in enumerate((1e-5, 1e-6)):
                pool.wait_ge(x8_stats, i + 1)
                ln_small(st8[:, :, :], mu8[:, :], rs8[:, :], t81[:, :], t82[:, :], eps)
                pool.tensor_copy(t81[:, :], t82[:, :]).then_inc(x8_small, 1)

            pool.wait_ge(stats_done, 1)
            znorm()
            centre(0)
            pool.wait_ge(zc_done, 1)
            scale()
            pool.wait_ge(mask_ready, 1)
            split(0, 0, 0, split1_done)

            def body(b, p, f):
                if f["prep"]:
                    if f["tail"]:
                        wait_ge(pv_done, NC * b)
                        wait_ge(e_done, NC * b)
                    rows = mbias[:, b + 1, :] if isinstance(b, int) else \
                        mbias[:, :, :].rearrange("p b c -> p (b c)")[:, bass.ds((b + 1) * NC, NC)]
                    pool.tensor_copy(mb[:, 1 - p, :], rows).then_inc(mb_done, 1)
                    split(b + 1, 1 - p, HC, split2_done)
                if f["znext"]:
                    wait_ge(stats_done, b + 3)
                    znorm()
                    wait_ge(split2_done, b + 2)
                    centre(p)
                    wait_ge(zc_done, b + 3)
                    scale()
                    if f["main"]:
                        wait_ge(pv_done, NC * b + HC)
                    split(b + 2, p, 0, split1_done)
                if f["tail"]:
                    wait_ge(rb_in, 16 * b)
                    if f["b_ge2"] and p == 1:
                        wait_ge(y_ready, b - 1)
                    pool.tensor_tensor(An[:, :, 1 - p, :], Af[:, :].rearrange("d (h n) -> d h n", n=NQ),
                                       Rb[:, :].rearrange("d (h n) -> d h n", n=NQ), ALU.mult).then_inc(an_done, 1)
                if f["wexp"]:
                    for e in f["wexp"]:
                        split_expert(e)

            LN_STEPS = 9
            PER = 2 + LN_STEPS + 1 + 2

            for b, ex in ((-1, ()), (0, (0, 1)), (1, (2, 3))):
                body(b, b % 2, dict(flags(b), wexp=ex))
            n0 = ch.n
            with pool.Fori(2, B - 3, 2) as i:
                ch.base, ch.n = PER * i - 2 * PER + n0, 0
                body(i, 0, STEADY[0])
                assert ch.n == PER
                body(i + 1, 1, STEADY[1])
                assert ch.n == 2 * PER
            ch.base, ch.n = 0, n0 + (B - 4) * PER
            for b, ex in ((B - 2, (4, 5)), (B - 1, ())):
                body(b, b % 2, dict(flags(b), wexp=ex))
            b = B
            wait_ge(rb_in, 16 * b)
            pool.tensor_tensor(An[:, :, 1, :], Af[:, :].rearrange("d (h n) -> d h n", n=NQ),
                               Rb[:, :].rearrange("d (h n) -> d h n", n=NQ), ALU.mult).then_inc(an_done, 1)
            split_expert(6)
            split_expert(7)
            for i, eps in ((2, 1e-6), (3, 1e-5)):
                wait_ge(x8_stats, i + 1)
                ln_small(st8[:, :, :], mu8[:, :], rs8[:, :], t81[:, :], t82[:, :], eps)
                pool.tensor_copy(t81[:, :], t82[:, :]).then_inc(x8_small, 1)

        @block.scalar
        def _(act):
            act.dma_start(idf[:, :], ident_f32).then_inc(ld_w, 16)
            act.dma_start(idh[:, :], ident_f16).then_inc(ld_w, 16)
            act.dma_start(cs[:, 0:1], lnc_s.rearrange("(p o) -> p o", o=1)).then_inc(ld_w, 16)
            act.dma_start(cs[:, 1:2], lnc_b.rearrange("(p o) -> p o", o=1)).then_inc(ld_w, 16)
            act.dma_start(l1[:, 0:1], ln1_s.rearrange("(p o) -> p o", o=1)).then_inc(ld_w, 16)
            act.dma_start(l1[:, 1:2], ln1_b.rearrange("(p o) -> p o", o=1)).then_inc(ld_w, 16)
            for half in range(2):
                for k in range(2):
                    act.dma_start(nkv[half * DH:(half + 1) * DH, k:k + 1],
                                  null_kv[k].rearrange("(d o) -> d o", o=1)).then_inc(ld_w, 16)
            act.dma_start(Wq_s[:, :], Wq).then_inc(ld_w, 16)
            act.dma_start(Wkv_s[:, :], Wkv).then_inc(ld_w, 16)
            act.dma_start(Wo_s[:, :, :], Wo.rearrange("(t p) n -> p t n", p=128)).then_inc(ld_w, 16)

            for s in range(6):
                dst = (WqT, WkT, WvT)[s // 2]
                act.wait_ge(wt_ready, s + 1)
                act.activation(dst[:, 4 * (s % 2):4 * (s % 2) + 4, :].rearrange("p t d -> p (t d)"),
                               X[:, s % 2, :], ACT.Copy, scale=ATT_SCALE if s < 2 else 1.0).then_inc(wt_copied, 1)
            for s in range(8):
                dst = (G, M)[s // 4]
                act.wait_ge(gm_ready, s + 1)
                h0 = 8 * (s % 4 // 2) + s % 2
                act.activation(dst[:, h0:h0 + 7:2, :], X[:, s % 2, :].rearrange("p (t d) -> p t d", d=D),
                               ACT.Copy).then_inc(gm_copied, 1)
            act.wait_ge(nv_ready, 1)
            act.activation(NVb[:, :], X[0:TT, 0, 0:D], ACT.Copy).then_inc(gm_copied, 1)

            for n, (dst, src) in enumerate((
                    (lno_r[:, 0, :], lno_s.rearrange("(o d) -> o d", o=1).partition_broadcast(TT)),
                    (lno_r[:, 1, :], lno_b.rearrange("(o d) -> o d", o=1).partition_broadcast(TT)),
                    (gates[:, 0:1], g_xattn.rearrange("(o d) -> o d", o=1).partition_broadcast(TT)),
                    (gates[:, 1:2], g_ffn.rearrange("(o d) -> o d", o=1).partition_broadcast(TT)),
                    (wr_s[:, :], wr), (br_r[:, :], br.rearrange("(o d) -> o d", o=1).partition_broadcast(TT)),
                    (b1_s[:, :], b1.rearrange("e (f p) -> (e f) p", p=128)), (b2_s[:, :], b2))):
                act.dma_start(dst, src).then_inc(ld_f, 16)

            def load_expert(e):
                if e >= 2:
                    act.wait_ge(wsplit, e - 1)
                act.dma_start(wst[:, e % 2, 0, :], w1[e]).then_inc(ld_we[e % 2], 16)
                act.dma_start(wst[:, e % 2, 1, :].rearrange("p (f d) -> p f d", d=D),
                              w2[e].rearrange("(f p) d -> p f d", p=128)).then_inc(ld_we[e % 2], 16)

            def exps(b, c, p):
                k = c % PB
                s = S[0:CK, 2 * (c % 2):2 * (c % 2) + 2, 0:HR]
                act.wait_ge(sim_done, NC * b + c + 1)
                if not (isinstance(b, int) and NC * b + c < PB):
                    act.wait_ge(pv_done, NC * b + c + 1 - PB)
                if c == 0:
                    act.wait_ge(mb_done, b + 1)
                act.activation(s, s, ACT.Exp, bias=mb[:, p, c:c + 1]).then_inc(e_done, 1)
                act.wait_ge(e_done, NC * b + c + 1)
                act.activation(Ph[:, k, :].rearrange("p (a r) -> p a r", a=2), s, ACT.Copy).then_inc(hi_done, 1)

            def zt_copy(nb, p, j):
                dst = (zTh, zTl)[j % 2]
                c0 = HC * CK * (j // 2)
                act.wait_ge(zt_ready, 4 * nb + j + 1)
                act.activation(dst[:, p, c0:c0 + HC * CK].rearrange("p (c k) -> p c k", k=CK),
                               XT[j % 2][:, :, 0:CK], ACT.Copy).then_inc(zt_copied, 1)

            def queries(n, p, n_ge1):
                for j in range(2):
                    act.wait_ge(q_ready, 2 * n + j + 1)
                    act.activation(qh[:, p, j * HR:(j + 1) * HR], X[:, j, 0:HR], ACT.Identity,
                                   scale=rowmask[:, 0:1], bias=rowbias[:, 0:1]).then_inc(qhi_done, 1)
                    if n_ge1 and j == 0:
                        act.wait_ge(null_in, 16 * n)
                    act.activation(nullrow[0:1, j * HR:(j + 1) * HR], X[0:1, j, 0:HR],
                                   ACT.Copy, scale=-1.0).then_inc(null_done, 1)

            def a_copy(b, b_ge1):
                act.wait_ge(pv_done, NC * b + NC)
                if b_ge1:
                    act.wait_ge(an_done, b)
                act.activation(Af[:, :].rearrange("d (a r) -> d a r", a=2), A[:, :, 0:HR], ACT.Copy).then_inc(a_copied, 1)

            def body(b, p, f):
                nb, np_ = b + 1, 1 - p
                for c in range(NC):
                    if c == 0 and f["tail"]:
                        a_copy(b - 1, f["b_ge2"])
                    if (f["main"] and c + 2 < NC) or (f["prep"] and c + 2 >= NC):
                        exps(*ahead(b, c), p if c + 2 < NC else np_)
                    if not f["prep"]:
                        continue
                    if c == 0:
                        zt_copy(nb, np_, 0)
                        zt_copy(nb, np_, 1)
                    if c == 1:
                        zt_copy(nb, np_, 2)
                        zt_copy(nb, np_, 3)
                    if c == 9:
                        act.wait_ge(mt_ready, nb + 1)
                        act.activation(qh[0:1, np_, :].rearrange("o (r t) -> o r t", t=RT),
                                       X[0:1, :, :].rearrange("o a r -> o (a r)")[:, 0:R]
                                       .rearrange("o (t r) -> o r t", t=RT), ACT.Copy).then_inc(slot_done, 1)
                        act.wait_ge(t7_done, nb + 1)
                        act.activation(P07[:, np_, :], t7[:, :], ACT.Exp).then_inc(p0_done, 1)
                    if c == 10 and f["znext"]:
                        queries(b + 2, p, True)

            load_expert(0)
            load_expert(1)
            act.wait_ge(b1_ready, 1)
            act.activation(b1T[:, :], X[:, 1, 0:E * FC], ACT.Copy).then_inc(b1_copied, 1)
            for e in (0, 1):
                act.wait_ge(xt_ready, e + 1)
                act.activation(xT[:, e * 4 * TT:(e + 1) * 4 * TT], X[:, e, 0:4 * TT], ACT.Identity,
                               scale=l1[:, 0:1], bias=l1[:, 1:2]).then_inc(xt_copied, 1)
            queries(0, 0, False)
            body(-1, 1, flags(-1))
            body(0, 0, flags(0))
            load_expert(2)
            load_expert(3)
            body(1, 1, flags(1))
            with act.Fori(2, B - 3, 2) as i:
                body(i, 0, STEADY[0])
                body(i + 1, 1, STEADY[1])
            load_expert(4)
            load_expert(5)
            body(B - 2, 0, flags(B - 2))
            body(B - 1, 1, flags(B - 1))
            a_copy(B - 1, True)
            load_expert(6)
            load_expert(7)
            act.wait_ge(ld_f, 16 * 8)
            act.activation(gates[:, :], gates[:, :], ACT.Tanh).then_inc(tanh_done, 1)

            for e in (0, 1):
                act.wait_ge(xt_ready, e + 3)
                act.activation(xT[:, e * 4 * TT:(e + 1) * 4 * TT], X[:, e, 0:4 * TT], ACT.Copy).then_inc(xt_copied, 1)

            act.wait_ge(ohT_ready, 1)
            act.activation(onehT[:, :, :].rearrange("e (a t) n -> e a (t n)", a=2), X[0:E, :, 0:4 * TT],
                           ACT.Copy).then_inc(ohT_copied, 1)

            def hidden(e, p):
                for f in range(FC):
                    g = FC * e + f
                    s = S[:, 2 * (f % 2):2 * (f % 2) + 2, 0:HR]
                    act.wait_ge(h_ready, g + 1)
                    if not (isinstance(e, int) and e < 2):
                        act.wait_ge(ye_ready, NT * (e - 1))
                    act.activation(gh[:, p, f, :].rearrange("p (a r) -> p a r", a=2), s, ACT.Gelu,
                                   scale=1.0 / W_SCALE, bias=b1T[:, bass.ds(g, 1)] if not isinstance(e, int)
                                   else b1T[:, g:g + 1]).then_inc(gh_done, 1)
                    act.wait_ge(gh_done, g + 1)
                    act.activation(s, s, ACT.Gelu, scale=1.0 / W_SCALE,
                                   bias=b1T[:, bass.ds(g, 1)] if not isinstance(e, int)
                                   else b1T[:, g:g + 1]).then_inc(gf_done, 1)

            for e in range(E):
                hidden(e, e % 2)

        @block.vector
        def _(dve):
            ch = Chain(dve_step, dve.wait_ge)

            def stats(dst, src, n, done):
                for c in range(n):
                    ins = dve.bn_stats(dst[:, c, :], src[:, c, :])
                ins.then_inc(done, 1)

            def wide8(v):
                return v.unsqueeze(2).broadcast_to([TT, NT, D])

            def normalise8(i, dst, src, done):
                stats(st8, src, NT, x8_stats)
                dve.wait_ge(x8_small, i + 1)
                ch.link(dve.tensor_tensor(dst[:, :, :], src[:, :, :], wide8(mu8[:, :]), ALU.subtract))
                ins = dve.tensor_tensor(dst[:, :, :], dst[:, :, :], wide8(rs8[:, :]), ALU.mult)
                ch.link(ins) if done is None else ins.then_inc(done, 1)

            dve.wait_ge(ld_ctx[0], 16)
            stats(st, raw[:, 0], NC, stats_done)
            dve.wait_ge(const_ready, 1)
            dve.wait_ge(ld_m, 16)
            ch.link(dve.tensor_copy(maskf[:, :, :], mask_s[:, :, :]))
            ch.link(dve.tensor_scalar(mbias[:, :, :], maskf[:, :, :], 1.0, MASK_BIAS, ALU.subtract, ALU.mult))
            dve.tensor_scalar(mcol[:, :, :], maskf[:, :, :], 1.0 - MASKED, MASKED, ALU.mult, ALU.add).then_inc(mask_ready, 1)
            dve.wait_ge(ld_w, 16 * 13)
            ch.link(dve.tensor_scalar(T[:, :], idf[:, :], cs[:, 0:1], None, ALU.mult))
            ch.link(dve.tensor_scalar(T[0:1, :], T[0:1, :], 0.0, cs[0:1, 0:1], ALU.mult, ALU.subtract))
            ch.link(dve.tensor_copy(T[:, 0:1], cs[:, 1:2]))
            dve.tensor_copy(nvrep[:, :], nkv[:, 1:2].broadcast_to([128, TT])).then_inc(t_ready, 1)
            dve.wait_ge(wt_copied, 6)
            ch.link(dve.tensor_scalar(WkT[:, :, 0], WkT[:, :, 0], -1.0, nkv[:, 0:1], ALU.mult, ALU.add))
            dve.tensor_scalar(WvT[:, :, 0], WvT[:, :, 0], nkv[:, 1:2], None, ALU.subtract).then_inc(fold_ready, 1)
            dve.wait_ge(ld_x, 16)
            normalise8(0, xn, x_s, None)
            normalise8(1, xn, xn, xt_in)

            def sub(b, c):
                k = c % PB
                dve.wait_ge(hi_done, NC * b + c + 1)
                dve.tensor_tensor(Pl[:, k, :].rearrange("p (a r) -> p a r", a=2),
                                  S[0:CK, 2 * (c % 2):2 * (c % 2) + 2, 0:HR],
                                  Ph[:, k, :].rearrange("p (a r) -> p a r", a=2), ALU.subtract).then_inc(lo_done, 1)

            def reciprocals(b):
                dve.wait_ge(s7_in, 16 * (b + 1))
                dve.wait_ge(p0_done, b + 1)
                pb = b_par[0]
                ch.link(dve.tensor_tensor(tot7[:, :], S7[:, :], P07[:, pb, :], ALU.add))
                dve.reciprocal(R7[:, :], tot7[:, :]).then_inc(r_done, 1)

            b_par = [0]

            def take_y(b):
                dve.wait_ge(y_ready, b)
                dst = y_s[:, :, :].rearrange("p t d -> p (t d)")
                lo_ = (b - 2) * (D // 2)
                v = dst[:, lo_:lo_ + D] if isinstance(b, int) else dst[:, bass.ds(lo_, D)]
                dve.tensor_tensor(v, X[0:TT, 0, 0:D], NVb[:, :], ALU.add).then_inc(y_done, 2)

            def queries(n, p):
                for j in range(2):
                    dve.wait_ge(null_done, 2 * n + j + 1)
                    dve.scalar_tensor_tensor(ql[:, p, j * HR:(j + 1) * HR], X[:, j, 0:HR], rowmask[:, 0:1],
                                             qh[:, p, j * HR:(j + 1) * HR], ALU.mult,
                                             ALU.subtract).then_inc(qlo_done, 1)

            def reduce(nb, j):
                blk, t = divmod(j, RT)
                dve.wait_ge(mx_ready, NMX * nb + j + 1)
                dve.reduce_max(mx3[:, t, blk:blk + 1], X[:, j % 2, 0:KB], AX).then_inc(mx_red, 1)

            def body(b, p, f):
                nb, np_ = b + 1, 1 - p
                for c in range(NC):
                    j0 = 3 * (c - 2)
                    maxima = f["prep"] and 2 <= c <= 8
                    if c == 0 and f["znext"]:
                        dve.wait_ge(zc_done, b + 2)
                        dve.wait_ge(ld_ctx[p], 16 * ((b - p) // 2) + 32 if isinstance(b, int) else (b - p) * 8 + 32)
                        for k in range(HC):
                            dve.bn_stats(st[:, k, :], raw[:, p, k, :])
                    if c == 1 and f["znext"]:
                        for k in range(HC, NC):
                            ins = dve.bn_stats(st[:, k, :], raw[:, p, k, :])
                        ins.then_inc(stats_done, 1)
                    if maxima:
                        reduce(nb, j0)
                        reduce(nb, j0 + 1)
                    if c == 9 and f["prep"]:
                        dve.wait_ge(mx_red, NMX * (nb + 1))
                        dve.wait_ge(null_in, 16 * (nb + 1))
                        ch.link(dve.tensor_reduce(negm[:, :], mx3[:, :, :], AX, ALU.max, negate=True))
                        ch.link(dve.scalar_tensor_tensor(negm[:, :], negm[:, :], -1.0, null7[:, :], ALU.add, ALU.min))
                        dve.tensor_scalar(mneg[:, :], negm[:, :], SHIFT - 1.0, None, ALU.add).then_inc(mneg_done, 1)
                        dve.wait_ge(mneg_done, nb + 1)
                        if f["prev"]:
                            dve.wait_ge(p0_done, nb)
                        dve.scalar_tensor_tensor(t7[:, :], mneg[:, :], 1.0, null7[:, :], ALU.add,
                                                 ALU.subtract).then_inc(t7_done, 1)
                    if c == NC - 1 and f["znext"]:
                        queries(b + 2, p)
                    if (f["main"] and c + 2 < NC) or (f["prep"] and c + 2 >= NC):
                        sub(*ahead(b, c))
                    if maxima:
                        reduce(nb, j0 + 2)
                    if c == 5 and f["tail"]:
                        b_par[0] = 1 - p
                        reciprocals(b - 1)
                    if c == NC - 1 and f["y"]:
                        take_y(b)

            queries(0, 0)
            for b in (-1, 0, 1):
                body(b, b % 2, flags(b))
            n0, PER = ch.n, 1 + 2
            with dve.Fori(2, B - 3, 2) as i:
                ch.base, ch.n = PER * i - 2 * PER + n0, 0
                body(i, 0, STEADY[0])
                assert ch.n == PER
                body(i + 1, 1, STEADY[1])
                assert ch.n == 2 * PER
            ch.base, ch.n = 0, n0 + (B - 4) * PER
            body(B - 2, 0, flags(B - 2))
            body(B - 1, 1, flags(B - 1))
            b_par[0] = 1
            reciprocals(B - 1)
            take_y(B)

            dve.wait_ge(y_done, B)
            normalise8(2, y_s, y_s, None)
            dve.wait_ge(tanh_done, 1)
            srow, brow = (lno_r[:, i, :].unsqueeze(1).broadcast_to([TT, NT, D]) for i in range(2))
            ch.link(dve.tensor_tensor(y_s[:, :, :], y_s[:, :, :], srow, ALU.mult))
            ch.link(dve.tensor_tensor(y_s[:, :, :], y_s[:, :, :], brow, ALU.add))
            ch.link(dve.scalar_tensor_tensor(x_s[:, :, :], y_s[:, :, :], gates[:, 0:1], x_s[:, :, :], ALU.mult, ALU.add))
            normalise8(3, xn, x_s, xt_in)
            for e in (0, 1):
                cols = slice(e * 4 * TT, (e + 1) * 4 * TT)
                dve.wait_ge(xt_copied, 3 + e)
                ch.link(dve.tensor_copy(xTh[:, cols], xT[:, cols]))
                dve.tensor_tensor(xTl[:, cols], xT[:, cols], xTh[:, cols], ALU.subtract).then_inc(xhl_done, 1)
            dve.wait_ge(sc_ready, 1)
            ch.link(dve.tensor_tensor(sc[:, :, :], A[0:TT, 0, 0:NT * E].rearrange("p (t e) -> p t e", e=E),
                                      br_r[:, :].unsqueeze(1).broadcast_to([TT, NT, E]), ALU.add))
            ch.link(dve.reduce_max(scm[:, :], sc[:, :, :], AX))
            ch.link(dve.tensor_tensor(eqm[:, :, :], sc[:, :, :], scm[:, :].unsqueeze(2).broadcast_to([TT, NT, E]), ALU.is_equal))
            erow_w = erow[:, :].unsqueeze(1).broadcast_to([TT, NT, E])
            ch.link(dve.tensor_tensor(eqm[:, :, :], eqm[:, :, :], erow_w, ALU.mult))
            ch.link(dve.tensor_reduce(esel[:, :], eqm[:, :, :], AX, ALU.min))
            ch.link(dve.tensor_tensor(oneh[:, :, :], erow_w, esel[:, :].unsqueeze(2).broadcast_to([TT, NT, E]), ALU.is_equal))
            dve.tensor_scalar(onehs[:, :, :], oneh[:, :, :], 1.0 / W_SCALE, None, ALU.mult).then_inc(oneh_done, 1)
            dve.wait_ge(acc0_ready, 1)
            dve.tensor_copy(moe[:, :, :].rearrange("p (a t) d -> p a (t d)", a=2), A[0:TT, :, :]).then_inc(acc0_copied, 1)
            dve.wait_ge(acc0_copied, 1)

            def low(e, p):
                for f in range(FC):
                    g = FC * e + f
                    dve.wait_ge(gf_done, g + 1)
                    dve.tensor_tensor(gl[:, p, f, :].rearrange("p (a r) -> p a r", a=2),
                                      S[:, 2 * (f % 2):2 * (f % 2) + 2, 0:HR],
                                      gh[:, p, f, :].rearrange("p (a r) -> p a r", a=2), ALU.subtract).then_inc(gl_done, 1)
                    if not (isinstance(e, int) and e == 0):
                        for t in (2 * f, 2 * f + 1):
                            gather(e - 1, t)

            YB = [A[0:TT, 0, 0:D], A[0:TT, 1, 0:D], X[0:TT, 0, 0:D], X[0:TT, 1, 0:D]]

            def gather(e, t):
                n = NT * e + t
                dve.wait_ge(ye_ready, n + 1)
                if n >= NT:
                    dve.wait_ge(ye_done, n - NT + 1)
                dve.scalar_tensor_tensor(moe[:, t, :], YB[t % 4], onehs[:, t, e:e + 1], moe[:, t, :],
                                         ALU.mult, ALU.add).then_inc(ye_done, 1)

            for e in range(E):
                low(e, e % 2)
            for t in range(NT):
                gather(E - 1, t)
            dve.wait_ge(ye_done, NT * E)
            dve.scalar_tensor_tensor(xn[:, :, :], moe[:, :, :], gates[:, 1:2], x_s[:, :, :], ALU.mult,
                                     ALU.add).then_inc(fin_done, 1)

        @block.tensor
        def _(pe):
            mm = pe.matmul
            pe.wait_ge(t_ready, 1)
            for s in range(6):
                if s >= 2:
                    pe.wait_ge(wt_copied, s - 1)
                for i in range(4):
                    t = 4 * (s % 2) + i
                    o = X[:, s % 2, i * D:(i + 1) * D]
                    if s < 2:
                        ins = pe.transpose(o, Wq_s[:, t * 128:(t + 1) * 128], idf[:, :])
                    else:
                        w0 = (s // 2 - 1) * INNER + t * 128
                        ins = mm(o, Wkv_s[:, w0:w0 + 128], T[:, :], start=True, stop=True)
                ins.then_inc(wt_ready, 1)
            pe.wait_ge(fold_ready, 1)
            for s in range(8):
                if s >= 2:
                    pe.wait_ge(gm_copied, s - 1)
                for i in range(4):
                    h = 8 * (s % 4 // 2) + s % 2 + 2 * i
                    r0 = DH * (h % 2)
                    lhs, rhs = (WqT, WkT) if s < 4 else (WvT, Wo_s)
                    ins = mm(X[:, s % 2, i * D:(i + 1) * D], lhs[r0:r0 + DH, h // 2, :], rhs[r0:r0 + DH, h // 2, :],
                             start=True, stop=True)
                ins.then_inc(gm_ready, 1)
            pe.wait_ge(gm_copied, 7)
            for t in range(NP):
                ins = mm(X[0:TT, 0, 0:D], nvrep[:, :], Wo_s[:, t, :], start=(t == 0), stop=(t == NP - 1))
            ins.then_inc(nv_ready, 1)
            pe.wait_ge(ld_f, 16 * 8)
            pe.wait_ge(gm_copied, 9)
            pe.transpose(X[:, 1, 0:E * FC], b1_s[:, :], idf[0:E * FC, 0:E * FC]).then_inc(b1_ready, 1)

            def transpose_tokens(i):
                pe.wait_ge(xt_in, i + 1)
                for a in range(2):
                    for t in range(4):
                        ins = pe.transpose(X[:, a, t * TT:(t + 1) * TT], xn[:, 4 * a + t, :], idf[0:TT, 0:TT])
                    ins.then_inc(xt_ready, 1)

            pe.wait_ge(b1_copied, 1)
            transpose_tokens(0)

            def sim(b, c, p):
                if c == 0:
                    pe.wait_ge(slot_done, b + 1)
                    pe.wait_ge(qlo_done, 2 * b + 2)
                    pe.wait_ge(zt_copied, 4 * b + 4)
                if not (isinstance(b, int) and NC * b + c < 2):
                    pe.wait_ge(lo_done, NC * b + c - 1)
                ks = slice(c * CK, (c + 1) * CK)
                for n, (z, q) in enumerate(((zTh, qh), (zTh, ql), (zTl, qh))):
                    for a in range(2):
                        ins = mm(S[0:CK, 2 * (c % 2) + a, 0:HR], z[:, p, ks], q[:, p, a * HR:(a + 1) * HR],
                                 start=(n == 0), stop=(n == 2))
                ins.then_inc(sim_done, 1)

            def pv(b, c, p, b_ge1, half):
                if c == 0 and half == 0 and b_ge1:
                    pe.wait_ge(a_copied, b)
                k, n = c % PB, 0
                if half == 0:
                    pe.wait_ge(hi_done, NC * b + c + 1)
                for z, q, a in ((zh, Ph, 0), (zh, Ph, 1), (zl, Ph, 0), (zl, Ph, 1), (zh, Pl, 0), (zh, Pl, 1)):
                    if n // 3 == half:
                        if n == 4:
                            pe.wait_ge(lo_done, NC * b + c + 1)
                        ins = mm(A[:, a, 0:HR], z[:, p, c, :], q[:, k, a * HR:(a + 1) * HR],
                                 start=(c == 0 and n < 2), stop=(c == NC - 1 and n >= 4))
                    n += 1
                if half == 1:
                    ins.then_inc(pv_done, 1)

            def zt(nb, p, j):
                z = (zh, zl)[j % 2]
                for i in range(HC):
                    ins = pe.transpose(XT[j % 2][:, i, 0:CK], z[:, p, HC * (j // 2) + i, :], idh[0:CK, 0:CK])
                ins.then_inc(zt_ready, 1)

            def queries(n, p, j, n_ge1):
                if n_ge1 and j == 0:
                    pe.wait_ge(slot_done, n)
                for i in range(H // 2):
                    h = j * (H // 2) + i
                    xs = xT[:, n * NQ:(n + 1) * NQ] if isinstance(n, int) else xT[:, bass.ds(n * NQ, NQ)]
                    ins = mm(X[:, j, i * NQ:(i + 1) * NQ], G[:, h, :], xs, start=True, stop=True)
                ins.then_inc(q_ready, 1)

            def aux(b, p, c, part, f):
                nb, np_ = b + 1, 1 - p
                if c == 0 and part < 2:
                    pe.wait_ge(qlo_done, 2 * nb + 1 + part)
                    if part == 0:
                        if f["t0y"]:
                            pe.wait_ge(y_done, b - 1)
                        pe.wait_ge(split1_done, nb + 1)
                    zt(nb, np_, part)
                if c == 1 and part < 2:
                    if part == 0:
                        pe.wait_ge(split2_done, nb + 1)
                    pe.wait_ge(zt_copied, 4 * nb + 1 + part)
                    zt(nb, np_, 2 + part)
                if 2 <= c <= 8:
                    j = 3 * (c - 2) + part
                    blk, t = divmod(j, RT)
                    if j < 2:
                        pe.wait_ge(zt_copied, 4 * nb + 3 + j)
                    else:
                        pe.wait_ge(mx_red, NMX * nb + j - 1)
                    mm(X[:, j % 2, 0:KB], qh[:, np_, t:R:RT], zTh[:, np_, blk * KB:(blk + 1) * KB],
                       start=True, stop=True).then_inc(mx_ready, 1)
                if c == 9 and part == 2:
                    pe.wait_ge(mneg_done, nb + 1)
                    for t in range(RT):
                        ins = mm(X[0:1, t // 4, (t % 4) * 128:(t % 4 + 1) * 128], mneg[:, t:t + 1], idh[:, :],
                                 start=True, stop=True)
                    ins.then_inc(mt_ready, 1)
                if c == 10 and part >= 1 and f["znext"]:
                    queries(b + 2, p, part - 1, True)

            def project(b):
                pe.wait_ge(an_done, b)
                for h in range(H):
                    ins = mm(X[0:TT, 0, 0:D], An[:, h, :, :].rearrange("d u n -> d (u n)"), M[:, h, :],
                             start=(h == 0), stop=(h == H - 1))
                ins.then_inc(y_ready, 2)

            def body(b, p, f):
                for c in range(NC):
                    scores = f["main"] if c + 2 < NC else f["prep"]
                    if c == 10 and f["main"]:
                        pv(b, c, p, f["tail"], 0)
                        pv(b, c, p, f["tail"], 1)
                    if scores:
                        sim(*ahead(b, c), p if c + 2 < NC else 1 - p)
                    for part in range(3):
                        if f["prep"]:
                            aux(b, p, c, part, f)
                        if f["main"] and c != 10 and part < 2:
                            pv(b, c, p, f["tail"], part)
                    if c == NC - 1 and f["y"]:
                        if f["znext"]:
                            pe.wait_ge(qlo_done, 2 * b + 5)
                        else:
                            pe.wait_ge(slot_done, b + 2)
                        project(b)

            pe.wait_ge(xt_copied, 2)
            queries(0, 0, 0, False)
            queries(0, 0, 1, False)
            iterate(pe, body, B - 2)
            pe.wait_ge(y_done, B - 2)
            project(B)

            pe.wait_ge(y_done, B)
            transpose_tokens(1)
            pe.wait_ge(xt_copied, 4)
            for t in range(NT):
                ins = mm(A[0:TT, 0, t * E:(t + 1) * E], xT[:, t * TT:(t + 1) * TT], wr_s[:, :], start=True, stop=True)
            ins.then_inc(sc_ready, 1)
            pe.wait_ge(xhl_done, 2)

            def up(e, f):
                g = FC * e + f
                if g >= 2:
                    pe.wait_ge(gl_done, g - 1)
                if f == 0:
                    pe.wait_ge(wsplit, e + 1)
                for n, (w, xx) in enumerate(((wh, xTh), (wh, xTl), (wl, xTh))):
                    for a in range(2):
                        ins = mm(S[:, 2 * (f % 2) + a, 0:HR], w[:, e, 0, f * 128:(f + 1) * 128],
                                 xx[:, a * HR:(a + 1) * HR], start=(n == 0), stop=(n == 2))
                ins.then_inc(h_ready, 1)

            YB = [A[0:TT, 0, 0:D], A[0:TT, 1, 0:D], X[0:TT, 0, 0:D], X[0:TT, 1, 0:D]]

            def down(e, p, t):
                n = NT * e + t
                if n >= 4:
                    pe.wait_ge(ye_done, n - 3)
                if t == 0:
                    pe.wait_ge(gl_done, FC * (e + 1))
                k = 0
                for f in range(FC):
                    for gg, w in ((gh, wh), (gl, wh), (gh, wl)):
                        ins = mm(YB[t % 4], gg[:, p, f, t * TT:(t + 1) * TT], w[:, e, 1, f * D:(f + 1) * D],
                                 start=(k == 0), stop=(k == 3 * FC - 1))
                        k += 1
                ins.then_inc(ye_ready, 1)

            up(0, 0)
            up(0, 1)
            pe.wait_ge(oneh_done, 1)
            for t in range(NT):
                ins = pe.transpose(X[0:E, t // 4, (t % 4) * TT:(t % 4 + 1) * TT], oneh[:, t, :], idf[0:TT, 0:TT])
            ins.then_inc(ohT_ready, 1)
            pe.wait_ge(ohT_copied, 1)
            for t in range(NT):
                ins = mm(A[0:TT, t // 4, (t % 4) * D:(t % 4 + 1) * D], onehT[:, t, :], b2_s[:, :], start=True, stop=True)
            ins.then_inc(acc0_ready, 1)
            pe.wait_ge(acc0_copied, 1)
            up(0, 2)
            up(0, 3)
            for e in range(1, E):
                for f in range(FC):
                    up(e, f)
                    down(e - 1, (e - 1) % 2, 2 * f)
                    down(e - 1, (e - 1) % 2, 2 * f + 1)
            for t in range(NT):
                down(E - 1, (E - 1) % 2, t)


_INS = ['x', 'ctx_1024', 'mask_BxS2_bf1', 'g_xattn', 'g_ffn', 'L0_xattn_ln1_s', 'L0_xattn_ln1_b', 'L0_xattn_lnc_s', 'L0_xattn_lnc_b',
        'L0_xattn_Wq', 'L0_xattn_Wkv', 'L0_xattn_null_kv', 'L0_xattn_Wo', 'L0_xattn_lno_s', 'L0_xattn_lno_b',
        'L0_ffn_wr', 'L0_ffn_br', 'L0_ffn_w1', 'L0_ffn_b1', 'L0_ffn_w2', 'L0_ffn_b2']


def kernel(**inputs):
    import numpy as _np
    import concourse.bacc as _bacc
    from concourse import mybir as _mybir
    from concourse.bass_utils import run_bass_kernel_spmd as _run

    nc = _bacc.Bacc("TRN2", target_bir_lowering=False, num_devices=1)
    arrays, args = {}, []

    def give(name, a):
        arrays[name] = a
        args.append(nc.dram_tensor(name, a.shape, _mybir.dt.from_np(a.dtype), kind="ExternalInput").ap())

    for name in _INS:
        a = _np.ascontiguousarray(inputs[name])
        give(f"in_{name}_dram", a.view(_np.uint8) if a.dtype == bool else a)
    give("ident_f32_dram", _np.eye(128, dtype=_np.float32))
    give("ident_f16_dram", _np.eye(128, dtype=_np.float16))
    args.append(nc.dram_tensor("out_dram", (16, 56, 128), _mybir.dt.float32, kind="ExternalOutput").ap())
    gated_cross_attention_moe_kernel(nc, *args)
    r = _run(nc, [arrays], core_ids=[0])
    return r.results[0]["out_dram"]
```

```python
import concourse.bass as bass
from concourse import mybir
from contextlib import ExitStack


def gated_cross_attention_moe_kernel(nc, x, ctx, mask, cols, rows, Wq, Wkv, Wo, wr, w1, b1, w2, b2,
                                     ident_f32, ident_f16, out):
    fp32, fp16 = mybir.dt.float32, mybir.dt.float16
    ALU = mybir.AluOpType
    ACT = mybir.ActivationFunctionType
    AX = mybir.AxisListType.X

    B, NQ, D = x.shape
    NKEY = ctx.shape[1]
    INNER = Wq.shape[1]
    H = 16
    DH = INNER // H
    NP = H // 2
    E, _, F = w1.shape
    FC = F // 128
    NC = 12
    CK = NKEY // NC
    R = H * NQ
    HR = R // 2
    RT = R // 128
    KB = NKEY // 3
    NMX = 3 * RT
    TT = 2 * NQ
    NT = B // 2
    NTOK = B * NQ
    GT = NT // 2
    NG = 2
    GTOK = GT * TT
    HC = NC // 2
    PB = 4
    ATT_SCALE = float(H) ** -0.5
    W_SCALE = 64.0
    SHIFT = 10 * 0.6931471805599453
    MASKED = 60000.0
    MASK_BIAS = 1.0e37
    TP = CK + 1

    ctx_v = ctx.rearrange("b (p c) d -> b p c d", c=NC)
    x_v = x.rearrange("(t u) n d -> (u n) t d", u=2)
    out_v = out.rearrange("(t u) n d -> (u n) t d", u=2)
    r_dram = nc.dram_tensor("r_scratch", (2, R), fp32, kind="Internal").ap()

    es = ExitStack()
    with es:
        def sb(name, shape, dt=fp32):
            return es.enter_context(nc.sbuf_tensor(name, shape, dt))

        def sem(name):
            return es.enter_context(nc.semaphore(name))

        raw = sb("raw", [CK, 2, NC, D])
        zf = sb("zf", [CK, NC, D])
        zh = sb("zh", [CK, 2, NC, D], fp16)
        zl = sb("zl", [CK, 2, NC, D], fp16)
        zTh = sb("zTh", [D, 2, NKEY], fp16)
        zTl = sb("zTl", [D, 2, NKEY], fp16)
        qh = sb("qh", [D, 2, R], fp16)
        ql = sb("ql", [D, 2, R], fp16)
        PP = sb("PP", [128, 2, PB, R], fp16)
        Ph, Pl = PP[0:CK, 0], PP[0:CK, 1]
        mask_s = sb("mask_s", [CK, B, NC], mybir.dt.uint8)
        maskf = sb("maskf", [CK, B, NC])
        mbias = sb("mbias", [CK, B, NC])
        mcol = sb("mcol", [CK, B, NC], fp16)
        mb = sb("mb", [CK, 2, NC])
        Af = sb("Af", [D, R])
        Rb = sb("Rb", [D, R])
        An = sb("An", [D, H, 2, NQ])
        Gh = sb("Gh", [D, H, D], fp16)
        Gl = sb("Gl", [D, H, D], fp16)
        M = sb("M", [D, H, D])
        st = sb("st", [CK, NC, 6])
        mu = sb("mu", [CK, NC])
        rs = sb("rs", [CK, NC])
        tmp1 = sb("tmp1", [CK, NC])
        tmp2 = sb("tmp2", [CK, NC])
        mhalf = sb("mhalf", [128, NC])
        nullrow = sb("nullrow", [1, R])
        null7 = sb("null7", [128, RT])
        mx3 = sb("mx3", [128, RT, 3])
        negm = sb("negm", [128, RT])
        mneg = sb("mneg", [128, RT], fp16)
        t7 = sb("t7", [128, RT])
        P07 = sb("P07", [128, 2, RT])
        S7 = sb("S7", [128, RT])
        tot7 = sb("tot7", [128, RT])
        R7 = sb("R7", [128, RT])
        idf = sb("idf", [128, 128])
        idh = sb("idh", [128, 128], fp16)
        T = sb("T", [D, D])
        rowmask = sb("rowmask", [D, 1])
        rowbias = sb("rowbias", [D, 1])
        cols_s = sb("cols_s", [128, 6])
        rows_s = sb("rows_s", [TT, 2 * D + E + 2])
        lnc_s, lnc_b, ln1_s, ln1_b, nk_c, nv_c = (cols_s[:, i:i + 1] for i in range(6))
        lno_s, lno_b = rows_s[:, 0:D], rows_s[:, D:2 * D]
        br_r, gates = rows_s[:, 2 * D:2 * D + E], rows_s[:, 2 * D + E:2 * D + E + 2]
        nvrep = sb("nvrep", [128, TT])
        NVb = sb("NVb", [TT, D])
        early = sb("early", [128, 3 * INNER])
        Wq_s = early[:, 0:INNER]
        Wkv_s = early[:, INNER:3 * INNER]
        NH = 2 * FC * GTOK
        gh = early[:, 0:NH // 2].bitcast(fp16).rearrange("p (a f n) -> p a f n", a=2, f=FC)
        gl = PP[:, :, :, :].rearrange("p i k r -> p (i k r)")[:, 0:NH].rearrange("p (a f n) -> p a f n", a=2, f=FC)
        Wo_s = sb("Wo_s", [128, NP, D])
        WqT = sb("WqT", [128, NP, D])
        WkT = sb("WkT", [128, NP, D])
        WvT = sb("WvT", [128, NP, D])
        x_s = sb("x_s", [TT, NT, D])
        y_s = sb("y_s", [TT, NT, D])
        xn = sb("xn", [TT, NT, D])
        st8 = sb("st8", [TT, NT, 6])
        mu8 = sb("mu8", [TT, NT])
        rs8 = sb("rs8", [TT, NT])
        t81 = sb("t81", [TT, NT])
        t82 = sb("t82", [TT, NT])
        xT = sb("xT", [D, NTOK])
        xTh = sb("xTh", [D, NTOK], fp16)
        xTl = sb("xTl", [D, NTOK], fp16)
        wr_s = sb("wr_s", [D, E])
        b1_s = sb("b1_s", [E * FC, 128])
        b1T = sb("b1T", [128, E * FC])
        b2_s = sb("b2_s", [E, D])
        sc = sb("sc", [TT, NT, E])
        scm = sb("scm", [TT, NT])
        eqm = sb("eqm", [TT, NT, E])
        erow = sb("erow", [TT, E])
        esel = sb("esel", [TT, NT])
        oneh = sb("oneh", [TT, NT, E])
        onehs = sb("onehs", [TT, NT, E])
        onehT = sb("onehT", [E, NT, TT])
        wst = sb("wst", [D, 2, 2, F])
        wh = sb("wh", [128, E, 2, F], fp16)
        wl = sb("wl", [128, E, 2, F], fp16)
        moe = sb("moe", [TT, NT, D])
        b2s = sb("b2s", [TT, GT, D])

        S = es.enter_context(nc.psum_tensor("S", [128, 4, 512], fp32))
        A = es.enter_context(nc.psum_tensor("A", [128, 2, 512], fp32))
        X = es.enter_context(nc.psum_tensor("X", [128, 2, 512], fp32))
        Xh = X[:, :, :].bitcast(fp16)
        XT = [Xh[:, i, 0:HC * TP].rearrange("p (c k) -> p c k", k=TP) for i in range(2)]

        ld_w = sem("ld_w")
        ld_x = sem("ld_x")
        ld_wo = sem("ld_wo")
        ld_c = sem("ld_c")
        ld_m = sem("ld_m")
        mask_ready = sem("mask_ready")
        ld_ctx = [sem("ld_ctx_even"), sem("ld_ctx_odd")]
        ld_f = sem("ld_f")
        ld_we = [sem("ld_we_even"), sem("ld_we_odd")]
        s7_in = sem("s7_in")
        null_in = sem("null_in")
        r_out = sem("r_out")
        rb_in = sem("rb_in")
        out_done = sem("out_done")
        dve_step = sem("dve_step")
        pool_step = sem("pool_step")
        pool_gate = sem("pool_gate")
        sp_gate = sem("sp_gate")
        const_ready = sem("const_ready")
        t_ready = sem("t_ready")
        wt_ready = sem("wt_ready")
        wt_copied = sem("wt_copied")
        fold_ready = sem("fold_ready")
        g_ready = sem("g_ready")
        ghi_done = sem("ghi_done")
        glo_done = sem("glo_done")
        m_ready = sem("m_ready")
        m_copied = sem("m_copied")
        c0_small = sem("c0_small")
        z0_done = sem("z0_done")
        nv_ready = sem("nv_ready")
        x8_stats = sem("x8_stats")
        x8_small = sem("x8_small")
        xt_in = sem("xt_in")
        xt_ready = sem("xt_ready")
        xt_copied = sem("xt_copied")
        sim_done = sem("sim_done")
        hi_done = sem("hi_done")
        e_done = sem("e_done")
        lo_done = sem("lo_done")
        pv_done = sem("pv_done")
        a_copied = sem("a_copied")
        zt_ready = sem("zt_ready")
        zt_copied = sem("zt_copied")
        q_ready = sem("q_ready")
        qhi_done = sem("qhi_done")
        qlo_done = sem("qlo_done")
        null_done = sem("null_done")
        mx_ready = sem("mx_ready")
        mx_red = sem("mx_red")
        mneg_done = sem("mneg_done")
        t7_done = sem("t7_done")
        p0_done = sem("p0_done")
        mt_ready = sem("mt_ready")
        slot_done = sem("slot_done")
        stats_done = sem("stats_done")
        zc_done = sem("zc_done")
        mb_done = sem("mb_done")
        split1_done = sem("split1_done")
        split2_done = sem("split2_done")
        r_done = sem("r_done")
        an_done = sem("an_done")
        y_ready = sem("y_ready")
        y_done = sem("y_done")
        wsplit = sem("wsplit")
        tanh_done = sem("tanh_done")
        b1_ready = sem("b1_ready")
        b1_copied = sem("b1_copied")
        sc_ready = sem("sc_ready")
        sc_copied = sem("sc_copied")
        xhl_done = sem("xhl_done")
        oneh_done = sem("oneh_done")
        ohT_ready = sem("ohT_ready")
        ohT_copied = sem("ohT_copied")
        b2_ready = sem("b2_ready")
        b2_copied = sem("b2_copied")
        moe_fin = sem("moe_fin")
        h_ready = sem("h_ready")
        gh_done = sem("gh_done")
        gf_done = sem("gf_done")
        gl_done = sem("gl_done")
        ye_ready = sem("ye_ready")
        ye_done = sem("ye_done")
        fin_done = sem("fin_done")

        class Chain:

            def __init__(self, s, wait_ge):
                self.sem, self.wait_ge, self.base, self.n = s, wait_ge, 0, 0

            def wait(self):
                self.wait_ge(self.sem, self.base + self.n)

            def link(self, ins):
                ins.then_inc(self.sem, 1)
                self.n += 1
                self.wait()

        def waiter(eng, gate):
            def wait_ge(s, value):
                eng.wait_ge(s, value)
                if not isinstance(value, int):
                    eng.sem_inc(gate, 1)
            return wait_ge

        def ahead(b, c):
            return (b, c + 2) if c + 2 < NC else (b + 1, c + 2 - NC)

        EXPERTS_SPLIT = {0: (0, 1), 1: (2, 3), B - 2: (4, 5), B - 1: (6, 7)}
        EXPERTS_LOADED = {0: (2, 3), 1: (4, 5), B - 2: (6, 7)}

        def flags(b):
            return dict(main=b >= 0, prep=b + 1 < B, znext=b + 2 < B, load=b + 3 < B,
                        tail=b >= 1, b_ge2=b >= 2, y=b >= 2 and b % 2 == 0, t0y=b >= 3 and b % 2 == 1,
                        prev=b >= 0, wexp=EXPERTS_SPLIT.get(b, ()), wload=EXPERTS_LOADED.get(b, ()),
                        group=b == B - 1)

        STEADY = [flags(4), flags(5)]
        for f_ in STEADY:
            f_["load"] = True

        def iterate(eng, body, last):
            for b in (-1, 0, 1):
                body(b, b % 2, flags(b))
            with eng.Fori(2, last - 1, 2) as i:
                body(i, 0, STEADY[0])
                body(i + 1, 1, STEADY[1])
            for b in range(last, B):
                body(b, b % 2, flags(b))

        block = es.enter_context(nc.Block())

        @block.sync
        def _(sp):
            sp.dma_start(x_s[:, :, :], x_v).then_inc(ld_x, 16)
            sp.dma_start(Wq_s, Wq).then_inc(ld_w, 16)
            sp.dma_start(Wkv_s, Wkv).then_inc(ld_w, 16)
            with nc.allow_non_contiguous_dma("the mask's 12-byte runs"):
                sp.dma_start(mask_s[:, :, :], mask.rearrange("b (p c) -> p b c", c=NC)).then_inc(ld_m, 16)
            sp.dma_start(raw[:, 1], ctx_v[1]).then_inc(ld_ctx[1], 16)
            sp.dma_start(Wo_s[:, :, :], Wo.rearrange("(t p) n -> p t n", p=128)).then_inc(ld_wo, 16)
            sp.dma_start(rows_s[:, :], rows.partition_broadcast(TT)).then_inc(ld_f, 16)
            for dst, src in ((wr_s[:, :], wr), (b1_s[:, :], b1.rearrange("e (f p) -> (e f) p", p=128)), (b2_s[:, :], b2)):
                sp.dma_start(dst, src).then_inc(ld_f, 16)

            def load_expert(e):
                if e >= 2:
                    sp.wait_ge(wsplit, e - 1)
                sp.dma_start(wst[:, e % 2, 0, :], w1[e]).then_inc(ld_we[e % 2], 16)
                sp.dma_start(wst[:, e % 2, 1, :].rearrange("p (f d) -> p f d", d=D),
                             w2[e].rearrange("(f p) d -> p f d", p=128)).then_inc(ld_we[e % 2], 16)

            load_expert(0)
            load_expert(1)

            wait_ge = waiter(sp, sp_gate)

            def move_null(n):
                wait_ge(null_done, 2 * n + 2)
                sp.dma_start(null7[:, :], nullrow[0:1, :].rearrange("o (r t) -> o r t", t=RT)).then_inc(null_in, 16)

            def body(b, p, f):
                if f["load"]:
                    wait_ge(zc_done, b + 2)
                    wait_ge(stats_done, b + 2)
                    sp.dma_start(raw[:, 1 - p], ctx_v[b + 3]).then_inc(ld_ctx[1 - p], 16)
                if f["tail"]:
                    wait_ge(a_copied, b)
                    if f["b_ge2"]:
                        wait_ge(r_done, b - 1)
                    sp.dma_start(S7[:, :], Af[0:1, :].rearrange("o (r t) -> o r t", t=RT)).then_inc(s7_in, 16)
                if f["tail"]:
                    wait_ge(r_done, b)
                    sp.dma_start(r_dram[0, :].rearrange("(r t) -> r t", t=RT), R7[:, :]).then_inc(r_out, 16)
                    wait_ge(r_out, 16 * b)
                    if f["b_ge2"]:
                        wait_ge(an_done, b - 1)
                    sp.dma_start(Rb[:, :], r_dram[0:1, :].partition_broadcast(128)).then_inc(rb_in, 16)
                if f["znext"]:
                    wait_ge(t7_done, b + 2)
                    move_null(b + 2)
                for e in f["wload"]:
                    load_expert(e)

            move_null(0)
            iterate(sp, body, B - 4)
            b = B
            sp.wait_ge(a_copied, b)
            sp.wait_ge(r_done, b - 1)
            sp.dma_start(S7[:, :], Af[0:1, :].rearrange("o (r t) -> o r t", t=RT)).then_inc(s7_in, 16)
            sp.wait_ge(r_done, b)
            sp.dma_start(r_dram[0, :].rearrange("(r t) -> r t", t=RT), R7[:, :]).then_inc(r_out, 16)
            sp.wait_ge(r_out, 16 * b)
            sp.wait_ge(an_done, b - 1)
            sp.dma_start(Rb[:, :], r_dram[0:1, :].partition_broadcast(128)).then_inc(rb_in, 16)
            for g in range(NG):
                sp.wait_ge(fin_done, g + 1)
                sp.dma_start(out_v[:, g * GT:(g + 1) * GT, :], xn[:, g * GT:(g + 1) * GT, :]).then_inc(out_done, 16)
            sp.wait_ge(out_done, 16 * NG)

        @block.gpsimd
        def _(pool):
            wait_ge = waiter(pool, pool_gate)
            ch = Chain(pool_step, wait_ge)

            def ln_small(s, m, r, t1, t2, eps, done=None):
                n = m.shape[1]
                ch.link(pool.tensor_tensor(t1, s[:, :, 1], s[:, :, 4], ALU.add))
                ch.link(pool.tensor_scalar(m, t1, 0.5, 0.0, ALU.mult, ALU.add))
                ch.link(pool.tensor_tensor(t1, s[:, :, 1], s[:, :, 4], ALU.subtract))
                ch.link(pool.tensor_tensor(t2, t1, t1, ALU.mult))
                ch.link(pool.tensor_scalar(t1, t2, D / 4.0, float(D) * eps, ALU.mult, ALU.add))
                ch.link(pool.tensor_tensor(t2, s[:, :, 2], s[:, :, 5], ALU.add))
                ch.link(pool.tensor_tensor(t2, t1, t2, ALU.add))
                ch.link(pool.tensor_scalar(t1, t2, 1.0 / D, 0.0, ALU.mult, ALU.add))
                ins = pool.tensor_tensor(r, t1, mhalf[0:m.shape[0], 0:n], ALU.pow)
                ins.then_inc(done, 1) if done else ch.link(ins)

            def wide(v):
                return v.unsqueeze(2).broadcast_to([CK, NC, D])

            def znorm():
                ln_small(st[:, :, :], mu[:, :], rs[:, :], tmp1[:, :], tmp2[:, :], 1e-6)

            def centre(p):
                ins = pool.tensor_tensor(zf[:, :, :], raw[:, p], wide(mu[:, :]), ALU.subtract)
                ins.then_inc(zc_done, 1)
                return ins

            def scale():
                ch.link(pool.tensor_tensor(zf[:, :, :], zf[:, :, :], wide(rs[:, :]), ALU.mult))

            def split(n, p, c0, done):
                cols = mcol[:, n, c0:c0 + HC] if isinstance(n, int) else \
                    mcol[:, :, :].rearrange("p b c -> p (b c)")[:, bass.ds(n * NC + c0, HC)]
                ch.link(pool.tensor_copy(zh[:, p, c0:c0 + HC, 0], cols))
                hi, lo, z = zh[:, p, c0:c0 + HC, 1:D], zl[:, p, c0:c0 + HC, 1:D], zf[:, c0:c0 + HC, 1:D]
                ch.link(pool.tensor_scalar(hi, z, 1.0, 0.0, ALU.mult, ALU.add))
                pool.tensor_tensor(lo, z, hi, ALU.subtract).then_inc(done, 1)

            def split_expert(e):
                w = wst[:, e % 2]
                pool.wait_ge(ld_we[e % 2], 32 * (e // 2 + 1))
                ch.link(pool.tensor_scalar(w, w, W_SCALE, 0.0, ALU.mult, ALU.add))
                ch.link(pool.tensor_scalar(wh[:, e], w, 1.0, 0.0, ALU.mult, ALU.add))
                pool.tensor_tensor(wl[:, e], w, wh[:, e], ALU.subtract).then_inc(wsplit, 1)

            pool.memset(mhalf[:, :], -0.5)
            pool.memset(zl[:, :, :, 0:1], 0.0)
            for e in range(E):
                pool.memset(erow[:, e:e + 1], float(e - E))
            ch.link(pool.memset(rowmask[:, :], 1.0 / W_SCALE))
            ch.link(pool.memset(rowmask[0:1, :], 0.0))
            ch.link(pool.memset(rowbias[:, :], 0.0))
            ch.link(pool.memset(rowbias[0:1, :], -1.0))
            pool.memset(T[0:1, :], 0.0).then_inc(const_ready, 1)

            def ln_tiles(i, eps, n):
                pool.wait_ge(x8_stats, i + 1)
                ln_small(st8[:, 0:n, :], mu8[:, 0:n], rs8[:, 0:n], t81[:, 0:n], t82[:, 0:n], eps, x8_small)

            ln_tiles(0, 1e-5, NT)
            pool.wait_ge(stats_done, 1)
            ln_small(st[:, :, :], mu[:, :], rs[:, :], tmp1[:, :], tmp2[:, :], 1e-6, c0_small)
            ln_tiles(1, 1e-6, NT)
            pool.wait_ge(mask_ready, 1)
            pool.wait_ge(z0_done, 1)
            split(0, 0, 0, split1_done)

            def body(b, p, f):
                if f["prep"]:
                    if f["tail"]:
                        wait_ge(pv_done, NC * b)
                        wait_ge(e_done, NC * b)
                    rows = mbias[:, b + 1, :] if isinstance(b, int) else \
                        mbias[:, :, :].rearrange("p b c -> p (b c)")[:, bass.ds((b + 1) * NC, NC)]
                    pool.tensor_copy(mb[:, 1 - p, :], rows).then_inc(mb_done, 1)
                    split(b + 1, 1 - p, HC, split2_done)
                if f["znext"]:
                    wait_ge(stats_done, b + 3)
                    znorm()
                    wait_ge(split2_done, b + 2)
                    centre(p)
                    wait_ge(zc_done, b + 3)
                    scale()
                    if f["main"]:
                        wait_ge(pv_done, NC * b + HC)
                    split(b + 2, p, 0, split1_done)
                if f["group"]:
                    ln_tiles(2, 1e-6, GT)
                    ln_tiles(3, 1e-5, GT)
                if f["tail"]:
                    wait_ge(rb_in, 16 * b)
                    if f["b_ge2"] and p == 1:
                        wait_ge(y_ready, b - 1)
                    pool.tensor_tensor(An[:, :, 1 - p, :], Af[:, :].rearrange("d (h n) -> d h n", n=NQ),
                                       Rb[:, :].rearrange("d (h n) -> d h n", n=NQ), ALU.mult).then_inc(an_done, 1)
                for e in f["wexp"]:
                    split_expert(e)

            LN_STEPS = 9
            PER = 2 + LN_STEPS + 1 + 2

            for b in (-1, 0, 1):
                body(b, b % 2, flags(b))
            n0 = ch.n
            with pool.Fori(2, B - 3, 2) as i:
                ch.base, ch.n = PER * i - 2 * PER + n0, 0
                body(i, 0, STEADY[0])
                assert ch.n == PER
                body(i + 1, 1, STEADY[1])
                assert ch.n == 2 * PER
            ch.base, ch.n = 0, n0 + (B - 4) * PER
            for b in (B - 2, B - 1):
                body(b, b % 2, flags(b))
            b = B
            wait_ge(rb_in, 16 * b)
            pool.tensor_tensor(An[:, :, 1, :], Af[:, :].rearrange("d (h n) -> d h n", n=NQ),
                               Rb[:, :].rearrange("d (h n) -> d h n", n=NQ), ALU.mult).then_inc(an_done, 1)
            ln_tiles(4, 1e-6, GT)
            ln_tiles(5, 1e-5, GT)

        @block.scalar
        def _(act):
            act.dma_start(cols_s[:, :], cols).then_inc(ld_c, 16)
            act.dma_start(idf[:, :], ident_f32).then_inc(ld_c, 16)
            act.dma_start(raw[:, 0], ctx_v[0]).then_inc(ld_ctx[0], 16)
            act.dma_start(idh[:, :], ident_f16).then_inc(ld_c, 16)

            for s in range(6):
                dst = (WqT, WkT, WvT)[s // 2]
                act.wait_ge(wt_ready, s + 1)
                act.activation(dst[:, 4 * (s % 2):4 * (s % 2) + 4, :].rearrange("p t d -> p (t d)"),
                               X[:, s % 2, :], ACT.Copy, scale=ATT_SCALE * W_SCALE if s < 2 else 1.0).then_inc(wt_copied, 1)
            for s in range(4):
                h0 = 8 * (s // 2) + s % 2
                act.wait_ge(g_ready, s + 1)
                act.activation(Gh[:, h0:h0 + 7:2, :], X[:, s % 2, :].rearrange("p (t d) -> p t d", d=D),
                               ACT.Copy).then_inc(ghi_done, 1)

            def xt_copy(i, scale, bias):
                act.wait_ge(xt_ready, i + 1)
                act.activation(xT[:, (i % 2) * GTOK:(i % 2 + 1) * GTOK], X[:, i % 2 if i < 2 else 1, 0:GTOK],
                               ACT.Identity, scale=scale, bias=bias).then_inc(xt_copied, 1)

            act.wait_ge(ld_c, 16 * 3)
            xt_copy(0, ln1_s, ln1_b)
            xt_copy(1, ln1_s, ln1_b)

            def exps(b, c, p):
                k = c % PB
                s = S[0:CK, 2 * (c % 2):2 * (c % 2) + 2, 0:HR]
                act.wait_ge(sim_done, NC * b + c + 1)
                if not (isinstance(b, int) and NC * b + c < PB):
                    act.wait_ge(pv_done, NC * b + c + 1 - PB)
                if c == 0:
                    act.wait_ge(mb_done, b + 1)
                act.activation(s, s, ACT.Exp, bias=mb[:, p, c:c + 1]).then_inc(e_done, 1)
                act.wait_ge(e_done, NC * b + c + 1)
                act.activation(Ph[:, k, :].rearrange("p (a r) -> p a r", a=2), s, ACT.Copy).then_inc(hi_done, 1)

            def zt_copy(nb, p, j):
                dst = (zTh, zTl)[j % 2]
                c0 = HC * CK * (j // 2)
                act.wait_ge(zt_ready, 4 * nb + j + 1)
                act.activation(dst[:, p, c0:c0 + HC * CK].rearrange("p (c k) -> p c k", k=CK),
                               XT[j % 2][:, :, 0:CK], ACT.Copy).then_inc(zt_copied, 1)

            def queries(n, p, n_ge1):
                for j in range(2):
                    act.wait_ge(q_ready, 2 * n + j + 1)
                    act.activation(qh[:, p, j * HR:(j + 1) * HR], X[:, j, 0:HR], ACT.Identity,
                                   scale=rowmask[:, 0:1], bias=rowbias[:, 0:1]).then_inc(qhi_done, 1)
                    if n_ge1 and j == 0:
                        act.wait_ge(null_in, 16 * n)
                    act.activation(nullrow[0:1, j * HR:(j + 1) * HR], X[0:1, j, 0:HR],
                                   ACT.Copy, scale=-1.0 / W_SCALE).then_inc(null_done, 1)

            def a_copy(b, b_ge1):
                act.wait_ge(pv_done, NC * b + NC)
                if b_ge1:
                    act.wait_ge(an_done, b)
                act.activation(Af[:, :].rearrange("d (a r) -> d a r", a=2), A[:, :, 0:HR], ACT.Copy).then_inc(a_copied, 1)

            def body(b, p, f):
                nb, np_ = b + 1, 1 - p
                for c in range(NC):
                    if c == 0 and f["tail"]:
                        a_copy(b - 1, f["b_ge2"])
                    if (f["main"] and c + 2 < NC) or (f["prep"] and c + 2 >= NC):
                        exps(*ahead(b, c), p if c + 2 < NC else np_)
                    if f["group"] and c == 8:
                        xt_copy(2, 1.0, 0.0)
                    if not f["prep"]:
                        continue
                    if c == 0:
                        zt_copy(nb, np_, 0)
                        zt_copy(nb, np_, 1)
                    if c == 1:
                        zt_copy(nb, np_, 2)
                        zt_copy(nb, np_, 3)
                    if c == 9:
                        act.wait_ge(mt_ready, nb + 1)
                        act.activation(qh[0:1, np_, :].rearrange("o (r t) -> o r t", t=RT),
                                       X[0:1, :, :].rearrange("o a r -> o (a r)")[:, 0:R]
                                       .rearrange("o (t r) -> o r t", t=RT), ACT.Copy).then_inc(slot_done, 1)
                        act.wait_ge(t7_done, nb + 1)
                        act.activation(P07[:, np_, :], t7[:, :], ACT.Exp).then_inc(p0_done, 1)
                    if c == 10 and f["znext"]:
                        queries(b + 2, p, True)

            queries(0, 0, False)
            for s in range(4):
                h0 = 8 * (s // 2) + s % 2
                act.wait_ge(m_ready, s + 1)
                act.activation(M[:, h0:h0 + 7:2, :], S[:, s % 2, :].rearrange("p (t d) -> p t d", d=D),
                               ACT.Copy).then_inc(m_copied, 1)
            act.wait_ge(nv_ready, 1)
            act.activation(NVb[:, :], S[0:TT, 2, 0:D], ACT.Copy).then_inc(m_copied, 1)
            act.wait_ge(b1_ready, 1)
            act.activation(b1T[:, :], S[:, 3, 0:E * FC], ACT.Copy).then_inc(b1_copied, 1)
            act.wait_ge(ld_f, 16 * 4)
            act.activation(gates, gates, ACT.Tanh).then_inc(tanh_done, 1)

            for b in (-1, 0, 1):
                body(b, b % 2, flags(b))
            with act.Fori(2, B - 3, 2) as i:
                body(i, 0, STEADY[0])
                body(i + 1, 1, STEADY[1])
            body(B - 2, 0, flags(B - 2))
            body(B - 1, 1, flags(B - 1))
            a_copy(B - 1, True)

            def hidden(n):
                e, p = n % E, n % 2
                for f in range(FC):
                    g = FC * n + f
                    s = S[:, g % 4, 0:GTOK]
                    act.wait_ge(h_ready, g + 1)
                    act.activation(s, s, ACT.Gelu, scale=1.0 / W_SCALE,
                                   bias=b1T[:, FC * e + f:FC * e + f + 1]).then_inc(gf_done, 1)
                    act.wait_ge(gf_done, g + 1)
                    if n >= 2:
                        act.wait_ge(ye_ready, GT * (n - 1))
                    act.activation(gh[:, p, f, :], s, ACT.Copy).then_inc(gh_done, 1)

            def one_hot_copy(g):
                act.wait_ge(ohT_ready, g + 1)
                act.activation(onehT[:, g * GT:(g + 1) * GT, :].rearrange("e t n -> e (t n)"), X[0:E, 1, 0:GTOK],
                               ACT.Copy).then_inc(ohT_copied, 1)

            def bias2_copy(g):
                act.wait_ge(b2_ready, g + 1)
                if g:
                    act.wait_ge(moe_fin, g)
                act.activation(b2s[:, :, :].rearrange("p t d -> p (t d)"), X[0:TT, 1, :], ACT.Copy).then_inc(b2_copied, 1)

            one_hot_copy(0)
            for n in range(NG * E):
                hidden(n)
                if n == 1:
                    bias2_copy(0)
                if n == 6:
                    xt_copy(3, 1.0, 0.0)
                if n == 9:
                    one_hot_copy(1)
                if n == 11:
                    bias2_copy(1)

        @block.vector
        def _(dve):
            ch = Chain(dve_step, dve.wait_ge)

            def stats(dst, src, n, done):
                for c in range(n):
                    ins = dve.bn_stats(dst[:, c, :], src[:, c, :])
                ins.then_inc(done, 1)

            def wide8(v, n=NT):
                return v.unsqueeze(2).broadcast_to([TT, n, D])

            def wide12(v):
                return v.unsqueeze(2).broadcast_to([CK, NC, D])

            def apply_norm(i, dst, src, n, done):
                dve.wait_ge(x8_small, i + 1)
                ch.link(dve.tensor_tensor(dst, src, wide8(mu8[:, 0:n], n), ALU.subtract))
                ins = dve.tensor_tensor(dst, dst, wide8(rs8[:, 0:n], n), ALU.mult)
                ch.link(ins) if done is None else ins.then_inc(done, 1)

            dve.wait_ge(ld_x, 16)
            stats(st8, x_s, NT, x8_stats)
            dve.wait_ge(ld_ctx[0], 16)
            stats(st, raw[:, 0], NC, stats_done)
            dve.wait_ge(const_ready, 1)
            dve.wait_ge(ld_c, 16 * 3)
            ch.link(dve.tensor_scalar(T[:, :], idf[:, :], lnc_s, None, ALU.mult))
            ch.link(dve.tensor_scalar(T[0:1, :], T[0:1, :], 0.0, lnc_s[0:1, :], ALU.mult, ALU.subtract))
            ch.link(dve.tensor_copy(T[:, 0:1], lnc_b))
            dve.tensor_copy(nvrep[:, :], nv_c.broadcast_to([128, TT])).then_inc(t_ready, 1)
            apply_norm(0, xn[:, :, :], x_s[:, :, :], NT, None)
            stats(st8, xn, NT, x8_stats)
            dve.wait_ge(ld_m, 16)
            ch.link(dve.tensor_copy(maskf[:, :, :], mask_s[:, :, :]))
            ch.link(dve.tensor_scalar(mbias[:, :, :], maskf[:, :, :], 1.0, MASK_BIAS, ALU.subtract, ALU.mult))
            dve.tensor_scalar(mcol[:, :, :], maskf[:, :, :], 1.0 - MASKED, MASKED, ALU.mult, ALU.add).then_inc(mask_ready, 1)
            dve.wait_ge(c0_small, 1)
            dve.tensor_tensor(zf[:, :, :], raw[:, 0], wide12(mu[:, :]), ALU.subtract).then_inc(zc_done, 1)
            dve.wait_ge(zc_done, 1)
            dve.tensor_tensor(zf[:, :, :], zf[:, :, :], wide12(rs[:, :]), ALU.mult).then_inc(z0_done, 1)
            apply_norm(1, xn[:, :, :], xn[:, :, :], NT, xt_in)
            dve.wait_ge(wt_copied, 6)
            ch.link(dve.tensor_scalar(WkT[:, :, 0], WkT[:, :, 0], -1.0, nk_c, ALU.mult, ALU.add))
            dve.tensor_scalar(WvT[:, :, 0], WvT[:, :, 0], nv_c, None, ALU.subtract).then_inc(fold_ready, 1)
            for s in range(4):
                h0 = 8 * (s // 2) + s % 2
                dve.wait_ge(ghi_done, s + 1)
                dve.tensor_tensor(Gl[:, h0:h0 + 7:2, :], X[:, s % 2, :].rearrange("p (t d) -> p t d", d=D),
                                  Gh[:, h0:h0 + 7:2, :], ALU.subtract).then_inc(glo_done, 1)

            def halves(i):
                cs = slice((i % 2) * GTOK, (i % 2 + 1) * GTOK)
                dve.wait_ge(xt_copied, i + 1)
                ch.link(dve.tensor_copy(xTh[:, cs], xT[:, cs]))
                dve.tensor_tensor(xTl[:, cs], xT[:, cs], xTh[:, cs], ALU.subtract).then_inc(xhl_done, 1)

            halves(0)
            halves(1)

            def residual(g):
                ts = slice(g * GT, (g + 1) * GT)
                y = y_s[:, ts, :]
                apply_norm(2 * g + 2, y, y, GT, None)
                dve.wait_ge(tanh_done, 1)
                ch.link(dve.tensor_tensor(y, y, lno_s.unsqueeze(1).broadcast_to([TT, GT, D]), ALU.mult))
                ch.link(dve.tensor_tensor(y, y, lno_b.unsqueeze(1).broadcast_to([TT, GT, D]), ALU.add))
                ch.link(dve.scalar_tensor_tensor(x_s[:, ts, :], y, gates[:, 0:1], x_s[:, ts, :], ALU.mult, ALU.add))
                stats(st8, x_s[:, ts, :], GT, x8_stats)

            def route(g):
                ts = slice(g * GT, (g + 1) * GT)
                scg, eq, oh = sc[:, ts, :], eqm[:, ts, :], oneh[:, ts, :]
                dve.wait_ge(sc_ready, g + 1)
                dve.tensor_tensor(scg, X[0:TT, 1, 0:GT * E].rearrange("p (t e) -> p t e", e=E),
                                  br_r.unsqueeze(1).broadcast_to([TT, GT, E]), ALU.add).then_inc(sc_copied, 1)
                dve.wait_ge(sc_copied, g + 1)
                ch.link(dve.reduce_max(scm[:, ts], scg, AX))
                ch.link(dve.tensor_tensor(eq, scg, scm[:, ts].unsqueeze(2).broadcast_to([TT, GT, E]), ALU.is_equal))
                erow_w = erow[:, :].unsqueeze(1).broadcast_to([TT, GT, E])
                ch.link(dve.tensor_tensor(eq, eq, erow_w, ALU.mult))
                ch.link(dve.tensor_reduce(esel[:, ts], eq, AX, ALU.min))
                ch.link(dve.tensor_tensor(oh, erow_w, esel[:, ts].unsqueeze(2).broadcast_to([TT, GT, E]), ALU.is_equal))
                dve.tensor_scalar(onehs[:, ts, :], oh, 1.0 / W_SCALE, None, ALU.mult).then_inc(oneh_done, 1)

            def sub(b, c):
                k = c % PB
                dve.wait_ge(hi_done, NC * b + c + 1)
                dve.tensor_tensor(Pl[:, k, :].rearrange("p (a r) -> p a r", a=2),
                                  S[0:CK, 2 * (c % 2):2 * (c % 2) + 2, 0:HR],
                                  Ph[:, k, :].rearrange("p (a r) -> p a r", a=2), ALU.subtract).then_inc(lo_done, 1)

            def reciprocals(b):
                dve.wait_ge(s7_in, 16 * (b + 1))
                dve.wait_ge(p0_done, b + 1)
                pb = b_par[0]
                ch.link(dve.tensor_tensor(tot7[:, :], S7[:, :], P07[:, pb, :], ALU.add))
                dve.reciprocal(R7[:, :], tot7[:, :]).then_inc(r_done, 1)

            b_par = [0]

            def take_y(b, bank):
                dve.wait_ge(y_ready, b)
                dst = y_s[:, :, :].rearrange("p t d -> p (t d)")
                lo_ = (b - 2) * (D // 2)
                v = dst[:, lo_:lo_ + D] if isinstance(b, int) else dst[:, bass.ds(lo_, D)]
                dve.tensor_tensor(v, X[0:TT, bank, 0:D], NVb[:, :], ALU.add).then_inc(y_done, 2)

            def queries(n, p):
                for j in range(2):
                    dve.wait_ge(null_done, 2 * n + j + 1)
                    dve.scalar_tensor_tensor(ql[:, p, j * HR:(j + 1) * HR], X[:, j, 0:HR], rowmask[:, 0:1],
                                             qh[:, p, j * HR:(j + 1) * HR], ALU.mult,
                                             ALU.subtract).then_inc(qlo_done, 1)

            def reduce(nb, j):
                blk, t = divmod(j, RT)
                dve.wait_ge(mx_ready, NMX * nb + j + 1)
                dve.reduce_max(mx3[:, t, blk:blk + 1], X[:, j % 2, 0:KB], AX).then_inc(mx_red, 1)

            def body(b, p, f):
                nb, np_ = b + 1, 1 - p
                for c in range(NC):
                    j0 = 3 * (c - 2)
                    maxima = f["prep"] and 2 <= c <= 8
                    if c == 0 and f["znext"]:
                        dve.wait_ge(zc_done, b + 2)
                        dve.wait_ge(ld_ctx[p], 16 * ((b - p) // 2) + 32 if isinstance(b, int) else (b - p) * 8 + 32)
                        for k in range(HC):
                            dve.bn_stats(st[:, k, :], raw[:, p, k, :])
                    if c == 1 and f["znext"]:
                        for k in range(HC, NC):
                            ins = dve.bn_stats(st[:, k, :], raw[:, p, k, :])
                        ins.then_inc(stats_done, 1)
                    if maxima:
                        reduce(nb, j0)
                        reduce(nb, j0 + 1)
                    if c == 9 and f["prep"]:
                        dve.wait_ge(mx_red, NMX * (nb + 1))
                        dve.wait_ge(null_in, 16 * (nb + 1))
                        ch.link(dve.tensor_reduce(negm[:, :], mx3[:, :, :], AX, ALU.max, negate=True))
                        ch.link(dve.scalar_tensor_tensor(negm[:, :], negm[:, :], -1.0, null7[:, :], ALU.add, ALU.min))
                        dve.tensor_scalar(mneg[:, :], negm[:, :], SHIFT - 1.0, None, ALU.add).then_inc(mneg_done, 1)
                        dve.wait_ge(mneg_done, nb + 1)
                        if f["prev"]:
                            dve.wait_ge(p0_done, nb)
                        dve.scalar_tensor_tensor(t7[:, :], mneg[:, :], 1.0, null7[:, :], ALU.add,
                                                 ALU.subtract).then_inc(t7_done, 1)
                    if c == NC - 1 and f["znext"]:
                        queries(b + 2, p)
                    if (f["main"] and c + 2 < NC) or (f["prep"] and c + 2 >= NC):
                        sub(*ahead(b, c))
                    if maxima:
                        reduce(nb, j0 + 2)
                    if f["group"]:
                        if c == 0:
                            dve.wait_ge(y_done, NT)
                            stats(st8, y_s[:, 0:GT, :], GT, x8_stats)
                        if c == 4:
                            residual(0)
                        if c == 6:
                            apply_norm(3, xn[:, 0:GT, :], x_s[:, 0:GT, :], GT, xt_in)
                        if c == 8:
                            halves(2)
                        if c == 10:
                            route(0)
                    if c == 5 and f["tail"]:
                        b_par[0] = 1 - p
                        reciprocals(b - 1)
                    if c == NC - 1 and f["y"]:
                        take_y(b, 0)

            queries(0, 0)
            for b in (-1, 0, 1):
                body(b, b % 2, flags(b))
            n0, PER = ch.n, 1 + 2
            with dve.Fori(2, B - 3, 2) as i:
                ch.base, ch.n = PER * i - 2 * PER + n0, 0
                body(i, 0, STEADY[0])
                assert ch.n == PER
                body(i + 1, 1, STEADY[1])
                assert ch.n == 2 * PER
            ch.base, ch.n = 0, n0 + (B - 4) * PER
            body(B - 2, 0, flags(B - 2))
            body(B - 1, 1, flags(B - 1))
            YB = [A[0:TT, 0, 0:D], A[0:TT, 1, 0:D], X[0:TT, 0, 0:D]]

            def gather(n, t):
                k, e = GT * n + t, n % E
                tile = (n // E) * GT + t
                dve.wait_ge(ye_ready, k + 1)
                if e == 0:
                    dve.tensor_scalar(moe[:, tile, :], YB[k % 3], onehs[:, tile, e:e + 1], None,
                                      ALU.mult).then_inc(ye_done, 1)
                else:
                    dve.wait_ge(ye_done, k - GT + 1)
                    dve.scalar_tensor_tensor(moe[:, tile, :], YB[k % 3], onehs[:, tile, e:e + 1], moe[:, tile, :],
                                             ALU.mult, ALU.add).then_inc(ye_done, 1)

            def low(n):
                for f in range(FC):
                    g = FC * n + f
                    if n == 0 and f == 0:
                        dve.wait_ge(pv_done, NC * B)
                    dve.wait_ge(gh_done, g + 1)
                    dve.tensor_tensor(gl[:, n % 2, f, :], S[:, g % 4, 0:GTOK], gh[:, n % 2, f, :],
                                      ALU.subtract).then_inc(gl_done, 1)
                    if n >= 1:
                        gather(n - 1, f)

            def finish(g):
                ts = slice(g * GT, (g + 1) * GT)
                dve.wait_ge(ye_done, GT * E * (g + 1))
                dve.wait_ge(b2_copied, g + 1)
                dve.tensor_tensor(moe[:, ts, :], moe[:, ts, :], b2s[:, :, :], ALU.add).then_inc(moe_fin, 1)
                dve.wait_ge(moe_fin, g + 1)
                dve.scalar_tensor_tensor(xn[:, ts, :], moe[:, ts, :], gates[:, 1:2], x_s[:, ts, :], ALU.mult,
                                         ALU.add).then_inc(fin_done, 1)

            for n in range(NG * E):
                low(n)
                if n == 0:
                    b_par[0] = 1
                    reciprocals(B - 1)
                if n == 3:
                    take_y(B, 1)
                    dve.wait_ge(y_done, B)
                    stats(st8, y_s[:, GT:NT, :], GT, x8_stats)
                if n == 4:
                    residual(1)
                if n == 5:
                    apply_norm(5, xn[:, GT:NT, :], x_s[:, GT:NT, :], GT, xt_in)
                if n == 6:
                    halves(3)
                if n == 7:
                    route(1)
                if n == 8:
                    finish(0)
            for t in range(GT):
                gather(NG * E - 1, t)
            finish(1)

        @block.tensor
        def _(pe):
            mm = pe.matmul
            pe.wait_ge(ld_w, 32)
            pe.wait_ge(t_ready, 1)
            for s in range(6):
                if s >= 2:
                    pe.wait_ge(wt_copied, s - 1)
                for i in range(4):
                    t = 4 * (s % 2) + i
                    o = X[:, s % 2, i * D:(i + 1) * D]
                    if s < 2:
                        ins = pe.transpose(o, Wq_s[:, t * 128:(t + 1) * 128], idf[:, :])
                    else:
                        w0 = (s // 2 - 1) * INNER + t * 128
                        ins = mm(o, Wkv_s[:, w0:w0 + 128], T[:, :], start=True, stop=True)
                ins.then_inc(wt_ready, 1)
            pe.wait_ge(fold_ready, 1)

            def head_products(s, lhs, rhs, bank):
                for i in range(4):
                    h = 8 * (s // 2) + s % 2 + 2 * i
                    r0 = DH * (h % 2)
                    ins = mm(bank[:, i * D:(i + 1) * D], lhs[r0:r0 + DH, h // 2, :], rhs[r0:r0 + DH, h // 2, :],
                             start=True, stop=True)
                return ins

            for s in range(4):
                if s >= 2:
                    pe.wait_ge(glo_done, s - 1)
                head_products(s, WqT, WkT, X[:, s % 2, :]).then_inc(g_ready, 1)

            def transpose_tokens(i, t0, bank):
                pe.wait_ge(xt_in, i + 1)
                for t in range(GT):
                    ins = pe.transpose(X[:, bank, t * TT:(t + 1) * TT], xn[:, t0 + t, :], idf[0:TT, 0:TT])
                ins.then_inc(xt_ready, 1)

            pe.wait_ge(glo_done, 4)
            transpose_tokens(0, 0, 0)
            transpose_tokens(0, GT, 1)

            def sim(b, c, p):
                if c == 0:
                    pe.wait_ge(slot_done, b + 1)
                    pe.wait_ge(qlo_done, 2 * b + 2)
                    pe.wait_ge(zt_copied, 4 * b + 4)
                if not (isinstance(b, int) and NC * b + c < 2):
                    pe.wait_ge(lo_done, NC * b + c - 1)
                ks = slice(c * CK, (c + 1) * CK)
                for n, (z, q) in enumerate(((zTh, qh), (zTh, ql), (zTl, qh))):
                    for a in range(2):
                        ins = mm(S[0:CK, 2 * (c % 2) + a, 0:HR], z[:, p, ks], q[:, p, a * HR:(a + 1) * HR],
                                 start=(n == 0), stop=(n == 2))
                ins.then_inc(sim_done, 1)

            def pv(b, c, p, b_ge1, half):
                if c == 0 and half == 0 and b_ge1:
                    pe.wait_ge(a_copied, b)
                k, n = c % PB, 0
                if half == 0:
                    pe.wait_ge(hi_done, NC * b + c + 1)
                for z, q, a in ((zh, Ph, 0), (zh, Ph, 1), (zl, Ph, 0), (zl, Ph, 1), (zh, Pl, 0), (zh, Pl, 1)):
                    if n // 3 == half:
                        if n == 4:
                            pe.wait_ge(lo_done, NC * b + c + 1)
                        ins = mm(A[:, a, 0:HR], z[:, p, c, :], q[:, k, a * HR:(a + 1) * HR],
                                 start=(c == 0 and n < 2), stop=(c == NC - 1 and n >= 4))
                    n += 1
                if half == 1:
                    ins.then_inc(pv_done, 1)

            def zt(nb, p, j):
                z = (zh, zl)[j % 2]
                for i in range(HC):
                    ins = pe.transpose(XT[j % 2][:, i, 0:CK], z[:, p, HC * (j // 2) + i, :], idh[0:CK, 0:CK])
                ins.then_inc(zt_ready, 1)

            def queries(n, p, j, n_ge1):
                if n_ge1 and j == 0:
                    pe.wait_ge(slot_done, n)
                xh, xl = (v[:, n * NQ:(n + 1) * NQ] if isinstance(n, int) else v[:, bass.ds(n * NQ, NQ)]
                          for v in (xTh, xTl))
                for i in range(H // 2):
                    h = j * (H // 2) + i
                    o = X[:, j, i * NQ:(i + 1) * NQ]
                    mm(o, Gh[:, h, :], xh, start=True, stop=False)
                    mm(o, Gh[:, h, :], xl, start=False, stop=False)
                    ins = mm(o, Gl[:, h, :], xh, start=False, stop=True)
                ins.then_inc(q_ready, 1)

            def aux(b, p, c, part, f):
                nb, np_ = b + 1, 1 - p
                if c == 0 and part < 2:
                    pe.wait_ge(qlo_done, 2 * nb + 1 + part)
                    if part == 0:
                        if f["t0y"]:
                            pe.wait_ge(y_done, b - 1)
                        pe.wait_ge(split1_done, nb + 1)
                    zt(nb, np_, part)
                if c == 1 and part < 2:
                    if part == 0:
                        pe.wait_ge(split2_done, nb + 1)
                    pe.wait_ge(zt_copied, 4 * nb + 1 + part)
                    zt(nb, np_, 2 + part)
                if 2 <= c <= 8:
                    j = 3 * (c - 2) + part
                    blk, t = divmod(j, RT)
                    if j < 2:
                        pe.wait_ge(zt_copied, 4 * nb + 3 + j)
                    else:
                        pe.wait_ge(mx_red, NMX * nb + j - 1)
                    mm(X[:, j % 2, 0:KB], qh[:, np_, t:R:RT], zTh[:, np_, blk * KB:(blk + 1) * KB],
                       start=True, stop=True).then_inc(mx_ready, 1)
                if c == 9 and part == 2:
                    pe.wait_ge(mneg_done, nb + 1)
                    for t in range(RT):
                        ins = mm(X[0:1, t // 4, (t % 4) * 128:(t % 4 + 1) * 128], mneg[:, t:t + 1], idh[:, :],
                                 start=True, stop=True)
                    ins.then_inc(mt_ready, 1)
                if c == 10 and part >= 1 and f["znext"]:
                    queries(b + 2, p, part - 1, True)

            def project(b, bank):
                pe.wait_ge(an_done, b)
                for h in range(H):
                    ins = mm(X[0:TT, bank, 0:D], An[:, h, :, :].rearrange("d u n -> d (u n)"), M[:, h, :],
                             start=(h == 0), stop=(h == H - 1))
                ins.then_inc(y_ready, 2)

            def body(b, p, f):
                for c in range(NC):
                    scores = f["main"] if c + 2 < NC else f["prep"]
                    if c == 10 and f["main"]:
                        pv(b, c, p, f["tail"], 0)
                        pv(b, c, p, f["tail"], 1)
                    if scores:
                        sim(*ahead(b, c), p if c + 2 < NC else 1 - p)
                    for part in range(3):
                        if f["prep"]:
                            aux(b, p, c, part, f)
                        if f["main"] and c != 10 and part < 2:
                            pv(b, c, p, f["tail"], part)
                    if f["group"]:
                        if c == 7:
                            transpose_tokens(1, 0, 1)
                        if c == 9:
                            route(0)
                        if c == NC - 1:
                            for k in range(FC):
                                up(0, k)
                            one_hot(0)
                    if c == NC - 1 and f["y"]:
                        if f["znext"]:
                            pe.wait_ge(qlo_done, 2 * b + 5)
                        else:
                            pe.wait_ge(slot_done, b + 2)
                        project(b, 0)

            def route(g):
                pe.wait_ge(xt_copied, g + 3)
                for t in range(GT):
                    tile = g * GT + t
                    ins = mm(X[0:TT, 1, t * E:(t + 1) * E], xT[:, tile * TT:(tile + 1) * TT], wr_s[:, :], start=True, stop=True)
                ins.then_inc(sc_ready, 1)

            def one_hot(g):
                pe.wait_ge(oneh_done, g + 1)
                for t in range(GT):
                    ins = pe.transpose(X[0:E, 1, t * TT:(t + 1) * TT], oneh[:, g * GT + t, :], idf[0:TT, 0:TT])
                ins.then_inc(ohT_ready, 1)

            def bias2(g):
                pe.wait_ge(ohT_copied, g + 1)
                for t in range(GT):
                    ins = mm(X[0:TT, 1, t * D:(t + 1) * D], onehT[:, g * GT + t, :], b2_s[:, :], start=True, stop=True)
                ins.then_inc(b2_ready, 1)

            def up(n, f):
                g, e = FC * n + f, n % E
                if g < 4:
                    pe.wait_ge(lo_done, NC * B)
                else:
                    pe.wait_ge(gl_done, g - 3)
                if f == 0:
                    pe.wait_ge(wsplit, e + 1)
                    pe.wait_ge(xhl_done, 3 + n // E)
                xs = slice((n // E) * GTOK, (n // E + 1) * GTOK)
                for i, (w, xx) in enumerate(((wh, xTh), (wh, xTl), (wl, xTh))):
                    ins = mm(S[:, g % 4, 0:GTOK], w[:, e, 0, f * 128:(f + 1) * 128], xx[:, xs],
                             start=(i == 0), stop=(i == 2))
                ins.then_inc(h_ready, 1)

            YB = [A[0:TT, 0, 0:D], A[0:TT, 1, 0:D], X[0:TT, 0, 0:D]]

            def down(n, t):
                k, e, p = GT * n + t, n % E, n % 2
                if k == 0:
                    pe.wait_ge(a_copied, B)
                if k >= 3:
                    pe.wait_ge(ye_done, k - 2)
                if t == 0:
                    pe.wait_ge(gl_done, FC * (n + 1))
                i = 0
                for f in range(FC):
                    for gg, w in ((gh, wh), (gl, wh), (gh, wl)):
                        ins = mm(YB[k % 3], gg[:, p, f, t * TT:(t + 1) * TT], w[:, e, 1, f * D:(f + 1) * D],
                                 start=(i == 0), stop=(i == 3 * FC - 1))
                        i += 1
                ins.then_inc(ye_ready, 1)

            pe.wait_ge(xhl_done, 2)
            queries(0, 0, 0, False)
            queries(0, 0, 1, False)
            pe.wait_ge(ld_wo, 16)
            for s in range(4):
                if s >= 2:
                    pe.wait_ge(m_copied, s - 1)
                head_products(s, WvT, Wo_s, S[:, s % 2, :]).then_inc(m_ready, 1)
            for t in range(NP):
                ins = mm(S[0:TT, 2, 0:D], nvrep[:, :], Wo_s[:, t, :], start=(t == 0), stop=(t == NP - 1))
            ins.then_inc(nv_ready, 1)
            pe.wait_ge(ld_f, 16 * 4)
            pe.transpose(S[:, 3, 0:E * FC], b1_s[:, :], idf[0:E * FC, 0:E * FC]).then_inc(b1_ready, 1)
            pe.wait_ge(m_copied, 5)
            pe.wait_ge(b1_copied, 1)

            iterate(pe, body, B - 2)

            for n in range(NG * E):
                for f in range(FC):
                    if n + 1 < NG * E:
                        up(n + 1, f)
                    down(n, f)
                if n == 0:
                    bias2(0)
                if n == 2:
                    pe.wait_ge(b2_copied, 1)
                    project(B, 1)
                if n == 5:
                    pe.wait_ge(y_done, B)
                    transpose_tokens(2, GT, 1)
                if n == 6:
                    route(1)
                if n == 8:
                    one_hot(1)
                if n == 10:
                    bias2(1)


_INS = ['Wq', 'Wkv', 'Wo', 'wr', 'w1', 'b1', 'w2', 'b2']


def kernel(**inputs):
    import numpy as _np
    import concourse.bacc as _bacc
    from concourse import mybir as _mybir
    from concourse.bass_utils import run_bass_kernel_spmd as _run

    nc = _bacc.Bacc("TRN2", target_bir_lowering=False, num_devices=1)
    arrays, args = {}, []

    def give(name, a):
        arrays[name] = a
        args.append(nc.dram_tensor(name, a.shape, _mybir.dt.from_np(a.dtype), kind="ExternalInput").ap())

    give("x_dram", _np.ascontiguousarray(inputs["x"]))
    give("ctx_dram", _np.ascontiguousarray(inputs["ctx_1024"]))
    give("mask_dram", _np.ascontiguousarray(inputs["mask_BxS2_bf1"]).view(_np.uint8))
    nk, nv = _np.asarray(inputs["L0_xattn_null_kv"])
    give("cols_dram", _np.stack([inputs["L0_xattn_lnc_s"], inputs["L0_xattn_lnc_b"], inputs["L0_xattn_ln1_s"],
                                 inputs["L0_xattn_ln1_b"], _np.tile(nk, 2), _np.tile(nv, 2)], axis=1))
    give("rows_dram", _np.concatenate([inputs["L0_xattn_lno_s"], inputs["L0_xattn_lno_b"], inputs["L0_ffn_br"],
                                       inputs["g_xattn"], inputs["g_ffn"]])[None, :])
    for name in _INS:
        full = ("L0_xattn_" if name[0] == "W" else "L0_ffn_") + name
        give(f"in_{name}_dram", _np.ascontiguousarray(inputs[full]))
    give("ident_f32_dram", _np.eye(128, dtype=_np.float32))
    give("ident_f16_dram", _np.eye(128, dtype=_np.float16))
    args.append(nc.dram_tensor("out_dram", (16, 56, 128), _mybir.dt.float32, kind="ExternalOutput").ap())
    gated_cross_attention_moe_kernel(nc, *args)
    r = _run(nc, [arrays], core_ids=[0])
    return r.results[0]["out_dram"]
```

```python
import concourse.bass as bass
from concourse import mybir
from contextlib import ExitStack


def gated_cross_attention_moe_kernel(nc, x, ctx, mask, cols, rows, Wq, Wkv, Wo, wr, w1, b1, w2, b2,
                                     ident_f32, ident_f16, out):
    fp32, fp16 = mybir.dt.float32, mybir.dt.float16
    ALU = mybir.AluOpType
    ACT = mybir.ActivationFunctionType
    AX = mybir.AxisListType.X

    B, NQ, D = x.shape
    NKEY = ctx.shape[1]
    INNER = Wq.shape[1]
    H = 16
    DH = INNER // H
    NP = H // 2
    E, _, F = w1.shape
    FC = F // 128
    NC = 12
    CK = NKEY // NC
    R = H * NQ
    HR = R // 2
    RT = R // 128
    KB = NKEY // 3
    NMX = 3 * RT
    TT = 2 * NQ
    NT = B // 2
    NTOK = B * NQ
    GT = NT // 2
    NG = 2
    GTOK = GT * TT
    HC = NC // 2
    PB = 4
    ATT_SCALE = float(H) ** -0.5
    W_SCALE = 64.0
    SHIFT = 10 * 0.6931471805599453
    MASKED = 60000.0
    MASK_BIAS = 1.0e37
    TP = CK + 1

    ctx_v = ctx.rearrange("b (p c) d -> b p c d", c=NC)
    x_v = x.rearrange("(t u) n d -> (u n) t d", u=2)
    out_v = out.rearrange("(t u) n d -> (u n) t d", u=2)
    r_dram = nc.dram_tensor("r_scratch", (2, R), fp32, kind="Internal").ap()

    es = ExitStack()
    with es:
        def sb(name, shape, dt=fp32):
            return es.enter_context(nc.sbuf_tensor(name, shape, dt))

        def sem(name):
            return es.enter_context(nc.semaphore(name))

        raw = sb("raw", [CK, 2, NC, D])
        zf = sb("zf", [CK, NC, D])
        zh = sb("zh", [CK, 2, NC, D], fp16)
        zl = sb("zl", [CK, 2, NC, D], fp16)
        zTh = sb("zTh", [D, 2, NKEY], fp16)
        zTl = sb("zTl", [D, 2, NKEY], fp16)
        qh = sb("qh", [D, 2, R], fp16)
        ql = sb("ql", [D, 2, R], fp16)
        PP = sb("PP", [128, 2, PB, R], fp16)
        Ph, Pl = PP[0:CK, 0], PP[0:CK, 1]
        mask_s = sb("mask_s", [CK, B, NC], mybir.dt.uint8)
        maskf = sb("maskf", [CK, B, NC])
        mbias = sb("mbias", [CK, B, NC])
        mcol = sb("mcol", [CK, B, NC], fp16)
        mb = sb("mb", [CK, 2, NC])
        Af = sb("Af", [D, R])
        Rb = sb("Rb", [D, R])
        An = sb("An", [D, H, NQ])
        Anh = sb("Anh", [D, H, 2, NQ], fp16)
        Anl = sb("Anl", [D, H, 2, NQ], fp16)
        Gh = sb("Gh", [D, H, D], fp16)
        Gl = sb("Gl", [D, H, D], fp16)
        Mh = sb("Mh", [D, H, D], fp16)
        Ml = sb("Ml", [D, H, D], fp16)
        st = sb("st", [CK, NC, 6])
        mu = sb("mu", [CK, NC])
        rs = sb("rs", [CK, NC])
        tmp1 = sb("tmp1", [CK, NC])
        tmp2 = sb("tmp2", [CK, NC])
        mhalf = sb("mhalf", [128, NC])
        nullrow = sb("nullrow", [1, R])
        null7 = sb("null7", [128, RT])
        null7s = sb("null7s", [128, RT])
        mx3 = sb("mx3", [128, RT, 3])
        negm = sb("negm", [128, RT])
        mneg = sb("mneg", [128, RT], fp16)
        t7 = sb("t7", [128, RT])
        P07 = sb("P07", [128, 2, RT])
        S7 = sb("S7", [128, RT])
        tot7 = sb("tot7", [128, RT])
        R7 = sb("R7", [128, RT])
        idf = sb("idf", [128, 128])
        idh = sb("idh", [128, 128], fp16)
        T = sb("T", [D, D])
        rowmask = sb("rowmask", [D, 1])
        rowbias = sb("rowbias", [D, 1])
        cols_s = sb("cols_s", [128, 6])
        rows_s = sb("rows_s", [TT, 2 * D + E + 2])
        lnc_s, lnc_b, ln1_s, ln1_b, nk_c, nv_c = (cols_s[:, i:i + 1] for i in range(6))
        lno_s, lno_b = rows_s[:, 0:D], rows_s[:, D:2 * D]
        br_r, gates = rows_s[:, 2 * D:2 * D + E], rows_s[:, 2 * D + E:2 * D + E + 2]
        nvrep = sb("nvrep", [128, TT])
        NVb = sb("NVb", [TT, D])
        early = sb("early", [128, 3 * INNER])
        M = early[:, 0:H * D].rearrange("p (h d) -> p h d", d=D)
        Wq_s = early[:, 0:INNER]
        Wkv_s = early[:, INNER:3 * INNER]
        NH = 2 * FC * GTOK
        gh = early[:, 0:NH // 2].bitcast(fp16).rearrange("p (a f n) -> p a f n", a=2, f=FC)
        gl = [v[:, :, :].rearrange("p h d -> p (h d)")[:, 0:NH // 2].rearrange("p (f n) -> p f n", f=FC)
              for v in (Gh, Gl)]
        Wo_s = sb("Wo_s", [128, NP, D])
        WqT = sb("WqT", [128, NP, D])
        WkT = sb("WkT", [128, NP, D])
        WvT = sb("WvT", [128, NP, D])
        x_s = sb("x_s", [TT, NT, D])
        y_s = sb("y_s", [TT, NT, D])
        xn = sb("xn", [TT, NT, D])
        st8 = sb("st8", [TT, NT, 6])
        mu8 = sb("mu8", [TT, NT])
        rs8 = sb("rs8", [TT, NT])
        t81 = sb("t81", [TT, NT])
        t82 = sb("t82", [TT, NT])
        xT = sb("xT", [D, NTOK])
        xTh = sb("xTh", [D, NTOK], fp16)
        xTl = sb("xTl", [D, NTOK], fp16)
        wr_s = sb("wr_s", [D, E])
        b1_s = sb("b1_s", [E * FC, 128])
        b1T = sb("b1T", [128, E * FC])
        b2_s = sb("b2_s", [E, D])
        sc = sb("sc", [TT, NT, E])
        scm = sb("scm", [TT, NT])
        eqm = sb("eqm", [TT, NT, E])
        erow = sb("erow", [TT, E])
        esel = sb("esel", [TT, NT])
        oneh = sb("oneh", [TT, NT, E])
        onehs = sb("onehs", [TT, NT, E])
        onehT = sb("onehT", [E, NT, TT])
        wst = sb("wst", [D, 2, 2, F])
        wh = sb("wh", [128, E, 2, F], fp16)
        wl = sb("wl", [128, E, 2, F], fp16)
        moe = sb("moe", [TT, NT, D])
        b2s = sb("b2s", [TT, GT, D])

        S = es.enter_context(nc.psum_tensor("S", [128, 4, 512], fp32))
        A = es.enter_context(nc.psum_tensor("A", [128, 2, 512], fp32))
        X = es.enter_context(nc.psum_tensor("X", [128, 2, 512], fp32))
        Xh = X[:, :, :].bitcast(fp16)
        XT = [Xh[:, i, 0:HC * TP].rearrange("p (c k) -> p c k", k=TP) for i in range(2)]

        ld_x = sem("ld_x")
        ld_wq = sem("ld_wq")
        ld_wk = sem("ld_wk")
        ld_wv = sem("ld_wv")
        ld_wo = sem("ld_wo")
        ld_cols = sem("ld_cols")
        ld_idf = sem("ld_idf")
        ld_idh = sem("ld_idh")
        ld_m = sem("ld_m")
        mask_ready = sem("mask_ready")
        ld_ctx = [sem("ld_ctx_even"), sem("ld_ctx_odd")]
        ld_f = sem("ld_f")
        ld_we = [sem("ld_we_even"), sem("ld_we_odd")]
        s7_in = sem("s7_in")
        null_in = sem("null_in")
        r_out = sem("r_out")
        rb_in = sem("rb_in")
        out_done = sem("out_done")
        dve_step = sem("dve_step")
        pool_step = sem("pool_step")
        pool_gate = sem("pool_gate")
        sp_gate = sem("sp_gate")
        const_ready = sem("const_ready")
        t_ready = sem("t_ready")
        wt_ready = sem("wt_ready")
        wt_copied = sem("wt_copied")
        fold_k = sem("fold_k")
        fold_v = sem("fold_v")
        g_ready = sem("g_ready")
        ghi_done = sem("ghi_done")
        glo_done = sem("glo_done")
        m_ready = sem("m_ready")
        m_split = sem("m_split")
        m_copied = sem("m_copied")
        c0_var = sem("c0_var")
        c0_rs = sem("c0_rs")
        z0_done = sem("z0_done")
        nv_ready = sem("nv_ready")
        x1_done = sem("x1_done")
        x8_stats = sem("x8_stats")
        x8_small = sem("x8_small")
        xt_in = sem("xt_in")
        xt_ready = sem("xt_ready")
        xt_copied = sem("xt_copied")
        sim_done = sem("sim_done")
        hi_done = sem("hi_done")
        e_done = sem("e_done")
        lo_done = sem("lo_done")
        pv_done = sem("pv_done")
        a_copied = sem("a_copied")
        zt_ready = sem("zt_ready")
        zth_copied = sem("zth_copied")
        ztl_copied = sem("ztl_copied")
        q_ready = sem("q_ready")
        qhi_done = sem("qhi_done")
        qlo_done = sem("qlo_done")
        null_done = sem("null_done")
        mx_ready = sem("mx_ready")
        mx_red = sem("mx_red")
        ns_done = sem("ns_done")
        mneg_done = sem("mneg_done")
        t7_done = sem("t7_done")
        p0_done = sem("p0_done")
        mt_ready = sem("mt_ready")
        slot_done = sem("slot_done")
        stats_done = sem("stats_done")
        zc_done = sem("zc_done")
        mb_done = sem("mb_done")
        split1_done = sem("split1_done")
        split2h_done = sem("split2h_done")
        split2_done = sem("split2_done")
        r_done = sem("r_done")
        an_done = sem("an_done")
        y_ready = sem("y_ready")
        y_done = sem("y_done")
        wsplit = sem("wsplit")
        tanh_done = sem("tanh_done")
        b1_ready = sem("b1_ready")
        b1_copied = sem("b1_copied")
        sc_ready = sem("sc_ready")
        sc_copied = sem("sc_copied")
        xhl_done = sem("xhl_done")
        oneh_done = sem("oneh_done")
        ohT_ready = sem("ohT_ready")
        ohT_copied = sem("ohT_copied")
        b2_ready = sem("b2_ready")
        b2_copied = sem("b2_copied")
        moe_fin = sem("moe_fin")
        h_ready = sem("h_ready")
        gh_done = sem("gh_done")
        gf_done = sem("gf_done")
        gl_done = sem("gl_done")
        ye_ready = sem("ye_ready")
        ye_done = sem("ye_done")
        fin_done = sem("fin_done")

        class Chain:

            def __init__(self, s, wait_ge):
                self.sem, self.wait_ge, self.base, self.n = s, wait_ge, 0, 0

            def wait(self):
                self.wait_ge(self.sem, self.base + self.n)

            def link(self, ins):
                ins.then_inc(self.sem, 1)
                self.n += 1
                self.wait()

        def waiter(eng, gate):
            def wait_ge(s, value):
                eng.wait_ge(s, value)
                if not isinstance(value, int):
                    eng.sem_inc(gate, 1)
            return wait_ge

        def ahead(b, c):
            return (b, c + 2) if c + 2 < NC else (b + 1, c + 2 - NC)

        Y_PE, Y_DVE, X1_DVE, XT_PE, XT_ACT = 9, 13, 22, 24, 29
        EXPERTS_SPLIT = {0: (0, 1), 1: (2, 3), B - 2: (4, 5), B - 1: (6, 7)}
        EXPERTS_LOADED = {0: (2, 3), 1: (4, 5), B - 2: (6, 7)}

        def flags(b):
            return dict(main=b >= 0, prep=b + 1 < B, znext=b + 2 < B, load=b + 3 < B,
                        tail=b >= 1, b_ge2=b >= 2, y=b >= 2 and b % 2 == 0, t0y=b >= 3 and b % 2 == 1,
                        prev=b >= 0, wexp=EXPERTS_SPLIT.get(b, ()), wload=EXPERTS_LOADED.get(b, ()),
                        group=b == B - 1)

        STEADY = [flags(4), flags(5)]
        for f_ in STEADY:
            f_["load"] = True

        def iterate(eng, body, last):
            for b in (-1, 0, 1):
                body(b, b % 2, flags(b))
            with eng.Fori(2, last - 1, 2) as i:
                body(i, 0, STEADY[0])
                body(i + 1, 1, STEADY[1])
            for b in range(last, B):
                body(b, b % 2, flags(b))

        block = es.enter_context(nc.Block())

        @block.sync
        def _(sp):
            sp.dma_start(x_s[:, :, :], x_v).then_inc(ld_x, 16)
            sp.dma_start(Wq_s, Wq).then_inc(ld_wq, 16)
            sp.dma_start(raw[:, 0], ctx_v[0]).then_inc(ld_ctx[0], 16)
            sp.dma_start(Wkv_s[:, 0:INNER], Wkv[:, 0:INNER]).then_inc(ld_wk, 16)
            with nc.allow_non_contiguous_dma("the mask's 12-byte runs"):
                sp.dma_start(mask_s[:, :, :], mask.rearrange("b (p c) -> p b c", c=NC)).then_inc(ld_m, 16)
            sp.dma_start(Wkv_s[:, INNER:2 * INNER], Wkv[:, INNER:2 * INNER]).then_inc(ld_wv, 16)
            sp.dma_start(raw[:, 1], ctx_v[1]).then_inc(ld_ctx[1], 16)
            sp.dma_start(Wo_s[:, :, :], Wo.rearrange("(t p) n -> p t n", p=128)).then_inc(ld_wo, 16)
            sp.dma_start(rows_s[:, :], rows.partition_broadcast(TT)).then_inc(ld_f, 16)
            for dst, src in ((wr_s[:, :], wr), (b1_s[:, :], b1.rearrange("e (f p) -> (e f) p", p=128)),
                             (b2_s[:, :], b2)):
                sp.dma_start(dst, src).then_inc(ld_f, 16)

            def load_expert(e):
                if e >= 2:
                    sp.wait_ge(wsplit, e - 1)
                sp.dma_start(wst[:, e % 2, 0, :], w1[e]).then_inc(ld_we[e % 2], 16)
                sp.dma_start(wst[:, e % 2, 1, :].rearrange("p (f d) -> p f d", d=D),
                             w2[e].rearrange("(f p) d -> p f d", p=128)).then_inc(ld_we[e % 2], 16)

            load_expert(0)
            load_expert(1)

            wait_ge = waiter(sp, sp_gate)

            def move_null(n):
                wait_ge(null_done, 2 * n + 2)
                sp.dma_start(null7[:, :], nullrow[0:1, :].rearrange("o (r t) -> o r t", t=RT)).then_inc(null_in, 16)

            def body(b, p, f):
                if f["load"]:
                    wait_ge(zc_done, b + 2)
                    wait_ge(stats_done, b + 2)
                    sp.dma_start(raw[:, 1 - p], ctx_v[b + 3]).then_inc(ld_ctx[1 - p], 16)
                if f["tail"]:
                    wait_ge(a_copied, b)
                    if f["b_ge2"]:
                        wait_ge(r_done, b - 1)
                    sp.dma_start(S7[:, :], Af[0:1, :].rearrange("o (r t) -> o r t", t=RT)).then_inc(s7_in, 16)
                if f["tail"]:
                    wait_ge(r_done, b)
                    sp.dma_start(r_dram[0, :].rearrange("(r t) -> r t", t=RT), R7[:, :]).then_inc(r_out, 16)
                    wait_ge(r_out, 16 * b)
                    if f["b_ge2"]:
                        wait_ge(an_done, b - 1)
                    sp.dma_start(Rb[:, :], r_dram[0:1, :].partition_broadcast(128)).then_inc(rb_in, 16)
                if f["znext"]:
                    wait_ge(t7_done, b + 2)
                    move_null(b + 2)
                for e in f["wload"]:
                    load_expert(e)

            move_null(0)
            iterate(sp, body, B - 4)
            b = B
            sp.wait_ge(a_copied, b)
            sp.wait_ge(r_done, b - 1)
            sp.dma_start(S7[:, :], Af[0:1, :].rearrange("o (r t) -> o r t", t=RT)).then_inc(s7_in, 16)
            sp.wait_ge(r_done, b)
            sp.dma_start(r_dram[0, :].rearrange("(r t) -> r t", t=RT), R7[:, :]).then_inc(r_out, 16)
            sp.wait_ge(r_out, 16 * b)
            sp.wait_ge(an_done, b - 1)
            sp.dma_start(Rb[:, :], r_dram[0:1, :].partition_broadcast(128)).then_inc(rb_in, 16)
            for g in range(NG):
                sp.wait_ge(fin_done, g + 1)
                sp.dma_start(out_v[:, g * GT:(g + 1) * GT, :], xn[:, g * GT:(g + 1) * GT, :]).then_inc(out_done, 16)
            sp.wait_ge(out_done, 16 * NG)

        @block.gpsimd
        def _(pool):
            wait_ge = waiter(pool, pool_gate)
            ch = Chain(pool_step, wait_ge)

            def ln_small(s, m, r, t1, t2, eps, done=None, gain=1.0):
                n = m.shape[1]
                ch.link(pool.tensor_tensor(t1, s[:, :, 1], s[:, :, 4], ALU.add))
                ch.link(pool.tensor_scalar(m, t1, 0.5, 0.0, ALU.mult, ALU.add))
                ch.link(pool.tensor_tensor(t1, s[:, :, 1], s[:, :, 4], ALU.subtract))
                ch.link(pool.tensor_tensor(t2, t1, t1, ALU.mult))
                ch.link(pool.tensor_scalar(t1, t2, D / 4.0, float(D) * eps, ALU.mult, ALU.add))
                ch.link(pool.tensor_tensor(t2, s[:, :, 2], s[:, :, 5], ALU.add))
                ch.link(pool.tensor_tensor(t2, t1, t2, ALU.add))
                ch.link(pool.tensor_scalar(t1, t2, gain / D, 0.0, ALU.mult, ALU.add))
                ins = pool.tensor_tensor(r, t1, mhalf[0:m.shape[0], 0:n], ALU.pow)
                ins.then_inc(done, 1) if done else ch.link(ins)

            def wide(v):
                return v.unsqueeze(2).broadcast_to([CK, NC, D])

            def znorm():
                ln_small(st[:, :, :], mu[:, :], rs[:, :], tmp1[:, :], tmp2[:, :], 1e-6)

            def centre(p):
                ins = pool.tensor_tensor(zf[:, :, :], raw[:, p], wide(mu[:, :]), ALU.subtract)
                ins.then_inc(zc_done, 1)
                return ins

            def scale():
                ch.link(pool.tensor_tensor(zf[:, :, :], zf[:, :, :], wide(rs[:, :]), ALU.mult))

            def split(n, p, c0, done, hi_done=None):
                cols = mcol[:, n, c0:c0 + HC] if isinstance(n, int) else \
                    mcol[:, :, :].rearrange("p b c -> p (b c)")[:, bass.ds(n * NC + c0, HC)]
                ch.link(pool.tensor_copy(zh[:, p, c0:c0 + HC, 0], cols))
                hi, lo, z = zh[:, p, c0:c0 + HC, 1:D], zl[:, p, c0:c0 + HC, 1:D], zf[:, c0:c0 + HC, 1:D]
                ins = pool.tensor_scalar(hi, z, 1.0, 0.0, ALU.mult, ALU.add)
                if hi_done:
                    ins.then_inc(hi_done, 1)
                    wait_ge(hi_done, n + 1)
                else:
                    ch.link(ins)
                pool.tensor_tensor(lo, z, hi, ALU.subtract).then_inc(done, 1)

            def normalise(u):
                ch.link(pool.tensor_tensor(An[:, :, :], Af[:, :].rearrange("d (h n) -> d h n", n=NQ),
                                           Rb[:, :].rearrange("d (h n) -> d h n", n=NQ), ALU.mult))
                ch.link(pool.tensor_scalar(Anh[:, :, u, :], An[:, :, :], 1.0, 0.0, ALU.mult, ALU.add))
                pool.tensor_tensor(Anl[:, :, u, :], An[:, :, :], Anh[:, :, u, :], ALU.subtract).then_inc(an_done, 1)

            def split_expert(e):
                w = wst[:, e % 2]
                pool.wait_ge(ld_we[e % 2], 32 * (e // 2 + 1))
                ch.link(pool.tensor_scalar(w, w, W_SCALE, 0.0, ALU.mult, ALU.add))
                ch.link(pool.tensor_scalar(wh[:, e], w, 1.0, 0.0, ALU.mult, ALU.add))
                pool.tensor_tensor(wl[:, e], w, wh[:, e], ALU.subtract).then_inc(wsplit, 1)

            pool.memset(mhalf[:, :], -0.5)
            pool.memset(zl[:, :, :, 0:1], 0.0)
            for e in range(E):
                pool.memset(erow[:, e:e + 1], float(e - E))
            ch.link(pool.memset(rowmask[:, :], 1.0 / W_SCALE))
            ch.link(pool.memset(rowmask[0:1, :], 0.0))
            ch.link(pool.memset(rowbias[:, :], 0.0))
            ch.link(pool.memset(rowbias[0:1, :], -1.0))
            pool.memset(T[0:1, :], 0.0).then_inc(const_ready, 1)

            def ln_tiles(i, eps, n, gain=1.0):
                pool.wait_ge(x8_stats, i + 1)
                ln_small(st8[:, 0:n, :], mu8[:, 0:n], rs8[:, 0:n], t81[:, 0:n], t82[:, 0:n], eps, x8_small, gain)

            e1, e2 = 1e-5, 1e-6
            ln_tiles(0, e1 * e2 / (1 + e2), NT, 1 + e2)
            pool.wait_ge(c0_var, 1)
            pool.tensor_tensor(rs[:, :], tmp1[:, :], mhalf[0:CK, 0:NC], ALU.pow).then_inc(c0_rs, 1)

            def halves(i, cs):
                pool.wait_ge(xt_copied, i + 1)
                ch.link(pool.tensor_scalar(xTh[:, cs], xT[:, cs], 1.0, 0.0, ALU.mult, ALU.add))
                pool.tensor_tensor(xTl[:, cs], xT[:, cs], xTh[:, cs], ALU.subtract).then_inc(xhl_done, 1)

            halves(0, slice(0, GTOK))
            halves(1, slice(GTOK, NTOK))
            pool.wait_ge(mask_ready, 1)
            pool.wait_ge(z0_done, 1)
            split(0, 0, HC, split2_done, split2h_done)
            pool.tensor_copy(mb[:, 0, :], mbias[:, 0, :]).then_inc(mb_done, 1)

            def body(b, p, f):
                if f["prep"] and f["main"]:
                    if f["tail"]:
                        wait_ge(pv_done, NC * b)
                        wait_ge(e_done, NC * b)
                    split(b + 1, 1 - p, HC, split2_done, split2h_done)
                    rows = mbias[:, b + 1, :] if isinstance(b, int) else \
                        mbias[:, :, :].rearrange("p b c -> p (b c)")[:, bass.ds((b + 1) * NC, NC)]
                    pool.tensor_copy(mb[:, 1 - p, :], rows).then_inc(mb_done, 1)
                if f["znext"]:
                    wait_ge(stats_done, b + 3)
                    znorm()
                    wait_ge(split2_done, b + 2)
                    centre(p)
                    wait_ge(zc_done, b + 3)
                    scale()
                    if f["main"]:
                        wait_ge(pv_done, NC * b + HC)
                    split(b + 2, p, 0, split1_done)
                if f["group"]:
                    ln_tiles(1, 1e-6, GT)
                    ln_tiles(2, 1e-5, GT)
                if f["tail"]:
                    wait_ge(rb_in, 16 * b)
                    if f["b_ge2"] and p == 1:
                        wait_ge(y_ready, b - 1)
                    normalise(1 - p)
                for e in f["wexp"]:
                    split_expert(e)

            LN_STEPS = 9
            PER = 1 + LN_STEPS + 1 + 2 + 2

            body(-1, 1, flags(-1))
            pool.wait_ge(m_copied, 4)
            ch.link(pool.tensor_scalar(Mh[:, :, :], M[:, :, :], 1.0, 0.0, ALU.mult, ALU.add))
            pool.tensor_tensor(Ml[:, :, :], M[:, :, :], Mh[:, :, :], ALU.subtract).then_inc(m_split, 1)
            for b in (0, 1):
                body(b, b % 2, flags(b))
            n0 = ch.n
            with pool.Fori(2, B - 3, 2) as i:
                ch.base, ch.n = PER * i - 2 * PER + n0, 0
                body(i, 0, STEADY[0])
                assert ch.n == PER
                body(i + 1, 1, STEADY[1])
                assert ch.n == 2 * PER
            ch.base, ch.n = 0, n0 + (B - 4) * PER
            for b in (B - 2, B - 1):
                body(b, b % 2, flags(b))
            b = B
            wait_ge(rb_in, 16 * b)
            normalise(1)
            ln_tiles(3, 1e-6, GT)
            pool.wait_ge(x8_small, 4)
            ts = slice(GT, NT)
            y, x1, xn1 = y_s[:, ts, :], x_s[:, ts, :], xn[:, ts, :]

            def tiles(v):
                return v.unsqueeze(2).broadcast_to([TT, GT, D])

            def features(v):
                return v.unsqueeze(1).broadcast_to([TT, GT, D])

            pool.wait_ge(tanh_done, 1)
            ch.link(pool.tensor_tensor(y, y, tiles(mu8[:, 0:GT]), ALU.subtract))
            ch.link(pool.tensor_tensor(y, y, tiles(rs8[:, 0:GT]), ALU.mult))
            ch.link(pool.tensor_tensor(y, y, features(lno_s), ALU.mult))
            ch.link(pool.tensor_tensor(y, y, features(lno_b), ALU.add))
            ch.link(pool.tensor_tensor(y, y, tiles(gates[:, 0:1].broadcast_to([TT, GT])), ALU.mult))
            pool.tensor_tensor(x1, x1, y, ALU.add).then_inc(x1_done, 1)
            ln_tiles(4, 1e-5, GT)
            pool.wait_ge(x8_small, 5)
            ch.link(pool.tensor_tensor(xn1, x1, tiles(mu8[:, 0:GT]), ALU.subtract))
            pool.tensor_tensor(xn1, xn1, tiles(rs8[:, 0:GT]), ALU.mult).then_inc(xt_in, 1)
            halves(3, slice(GTOK, NTOK))

        @block.scalar
        def _(act):
            act.dma_start(cols_s[:, :], cols).then_inc(ld_cols, 16)
            act.dma_start(idf[:, :], ident_f32).then_inc(ld_idf, 16)
            act.dma_start(idh[:, :], ident_f16).then_inc(ld_idh, 16)

            for s in range(6):
                dst = (WqT, WkT, WvT)[s // 2]
                act.wait_ge(wt_ready, s + 1)
                act.activation(dst[:, 4 * (s % 2):4 * (s % 2) + 4, :].rearrange("p t d -> p (t d)"),
                               X[:, s % 2, :], ACT.Copy,
                               scale=ATT_SCALE * W_SCALE if s < 2 else 1.0).then_inc(wt_copied, 1)

            def xt_copy(i, scale, bias):
                act.wait_ge(xt_ready, i + 1)
                act.activation(xT[:, (i % 2) * GTOK:(i % 2 + 1) * GTOK], (A[:, i] if i < 2 else X[:, 1])[:, 0:GTOK],
                               ACT.Identity, scale=scale, bias=bias).then_inc(xt_copied, 1)

            act.wait_ge(ld_cols, 16)
            xt_copy(0, ln1_s, ln1_b)
            xt_copy(1, ln1_s, ln1_b)
            for s in range(4):
                h0 = 8 * (s // 2) + s % 2
                act.wait_ge(g_ready, s + 1)
                act.activation(Gh[:, h0:h0 + 7:2, :], S[:, s, :].rearrange("p (t d) -> p t d", d=D),
                               ACT.Copy).then_inc(ghi_done, 1)

            def scores_of(c):
                return S[0:CK, 2 * (c % 2):2 * (c % 2) + 2, 0:HR]

            def exps(b, c, p):
                s = scores_of(c)
                act.wait_ge(sim_done, NC * b + c + 1)
                if not (isinstance(b, int) and NC * b + c < PB):
                    act.wait_ge(pv_done, NC * b + c + 1 - PB)
                if c == 0:
                    act.wait_ge(mb_done, b + 1)
                act.activation(s, s, ACT.Exp, bias=mb[:, p, c:c + 1]).then_inc(e_done, 1)

            def exps_hi(b, c):
                act.wait_ge(e_done, NC * b + c + 1)
                act.activation(Ph[:, c % PB, :].rearrange("p (a r) -> p a r", a=2), scores_of(c),
                               ACT.Copy).then_inc(hi_done, 1)

            def value_copy(k):
                h0 = 8 * (k // 2) + k % 2
                act.wait_ge(m_ready, k + 1)
                act.activation(M[:, h0:h0 + 7:2, :], A[:, k % 2, :].rearrange("p (t d) -> p t d", d=D),
                               ACT.Copy, scale=W_SCALE).then_inc(m_copied, 1)

            def zt_copy(nb, p, j):
                dst, done = ((zTh, zth_copied), (zTl, ztl_copied))[j % 2]
                c0 = HC * CK * (j // 2)
                act.wait_ge(zt_ready, 4 * nb + j + 1)
                act.activation(dst[:, p, c0:c0 + HC * CK].rearrange("p (c k) -> p c k", k=CK),
                               XT[j % 2][:, :, 0:CK], ACT.Copy).then_inc(done, 1)

            def queries(n, p, j):
                query_hi(n, p, j, X[:, j, 0:HR])
                if j == 0:
                    act.wait_ge(null_in, 16 * n)
                null_scores(j, X[0:1, j, 0:HR])

            def query_hi(n, p, j, bank):
                act.wait_ge(q_ready, 2 * n + j + 1)
                act.activation(qh[:, p, j * HR:(j + 1) * HR], bank, ACT.Identity,
                               scale=rowmask[:, 0:1], bias=rowbias[:, 0:1]).then_inc(qhi_done, 1)

            def null_scores(j, row):
                act.activation(nullrow[0:1, j * HR:(j + 1) * HR], row, ACT.Copy,
                               scale=-1.0 / W_SCALE).then_inc(null_done, 1)

            def body(b, p, f):
                nb, np_ = b + 1, 1 - p

                for c in range(NC):
                    exp_slot = (f["main"] and c + 2 < NC) or (f["prep"] and c + 2 >= NC)
                    shifts_early = c == 9 and f["prep"] and f["main"]
                    queries_early = c >= 10 and f["znext"] and f["main"] and (f["y"] or c == 11)
                    if c == 11 and not f["main"]:
                        queries(b + 2, p, 1)
                    if exp_slot:
                        exps(*ahead(b, c), p if c + 2 < NC else np_)
                    if shifts_early:
                        shifts(nb, np_)
                    if queries_early:
                        queries(b + 2, p, c - 10)
                    if exp_slot:
                        exps_hi(*ahead(b, c))
                    if c == 9 and not f["main"]:
                        shifts(nb, np_)
                    if c == 10 and not f["main"]:
                        act.wait_ge(nv_ready, 1)
                        act.activation(NVb[:, :], A[0:TT, 0, 0:D], ACT.Copy).then_inc(m_copied, 1)
                        act.wait_ge(b1_ready, 1)
                        act.activation(b1T[:, :], A[:, 1, 0:E * FC], ACT.Copy).then_inc(b1_copied, 1)
                    if c == 10 and f["znext"] and not queries_early:
                        queries(b + 2, p, 0)
                    if f["group"] and c == 9:
                        xt_copy(2, 1.0, 0.0)

            def shifts(nb, np_):
                act.wait_ge(mt_ready, nb + 1)
                act.activation(qh[0:1, np_, :].rearrange("o (r t) -> o r t", t=RT),
                               X[0:1, :, :].rearrange("o a r -> o (a r)")[:, 0:R]
                               .rearrange("o (t r) -> o r t", t=RT), ACT.Copy).then_inc(slot_done, 1)
                act.wait_ge(t7_done, nb + 1)
                act.activation(P07[:, np_, :], t7[:, :], ACT.Exp).then_inc(p0_done, 1)

            value_copy(0)
            for j in range(4):
                zt_copy(0, 0, j)
            for j in range(2):
                query_hi(0, 0, j, S[:, 2 + j, 0:HR])
            for j in range(2):
                null_scores(j, S[0:1, 2 + j, 0:HR])
            for k in range(1, 4):
                value_copy(k)
            act.wait_ge(ld_f, 16 * 4)
            act.activation(gates, gates, ACT.Tanh).then_inc(tanh_done, 1)
            body(-1, 1, flags(-1))
            for b in (0, 1):
                body(b, b % 2, flags(b))
            with act.Fori(2, B - 3, 2) as i:
                body(i, 0, STEADY[0])
                body(i + 1, 1, STEADY[1])
            body(B - 2, 0, flags(B - 2))
            body(B - 1, 1, flags(B - 1))

            def hidden(g):
                n, f = divmod(g, FC)
                s = S[:, g % 4, 0:GTOK]
                act.wait_ge(h_ready, g + 1)
                act.activation(s, s, ACT.Gelu, scale=1.0 / W_SCALE,
                               bias=b1T[:, FC * (n % E) + f:FC * (n % E) + f + 1]).then_inc(gf_done, 1)
                act.wait_ge(gf_done, g + 1)
                if n >= 2:
                    act.wait_ge(ye_ready, GT * (n - 1))
                act.activation(gh[:, n % 2, f, :], s, ACT.Copy).then_inc(gh_done, 1)

            def one_hot_copy(g):
                act.wait_ge(ohT_ready, g + 1)
                act.activation(onehT[:, g * GT:(g + 1) * GT, :].rearrange("e t n -> e (t n)"), X[0:E, 1, 0:GTOK],
                               ACT.Copy).then_inc(ohT_copied, 1)

            def bias2_copy(g):
                act.wait_ge(b2_ready, g + 1)
                if g:
                    act.wait_ge(moe_fin, g)
                act.activation(b2s[:, :, :].rearrange("p t d -> p (t d)"), X[0:TT, 1, :],
                               ACT.Copy).then_inc(b2_copied, 1)

            for g in range(NG * E * FC):
                if g == 5:
                    one_hot_copy(0)
                if g == 9:
                    bias2_copy(0)
                if g == XT_ACT:
                    xt_copy(3, 1.0, 0.0)
                if g == 39:
                    one_hot_copy(1)
                if g == 46:
                    bias2_copy(1)
                hidden(g)

        @block.vector
        def _(dve):
            ch = Chain(dve_step, dve.wait_ge)

            def stats(dst, src, n, done):
                for c in range(n):
                    ins = dve.bn_stats(dst[:, c, :], src[:, c, :])
                ins.then_inc(done, 1)

            def wide8(v, n=NT):
                return v.unsqueeze(2).broadcast_to([TT, n, D])

            def wide12(v):
                return v.unsqueeze(2).broadcast_to([CK, NC, D])

            def apply_norm(i, dst, src, n, done):
                dve.wait_ge(x8_small, i + 1)
                ch.link(dve.tensor_tensor(dst, src, wide8(mu8[:, 0:n], n), ALU.subtract))
                ins = dve.tensor_tensor(dst, dst, wide8(rs8[:, 0:n], n), ALU.mult)
                ch.link(ins) if done is None else ins.then_inc(done, 1)

            def build_t():
                dve.wait_ge(const_ready, 1)
                dve.wait_ge(ld_cols, 16)
                dve.wait_ge(ld_idf, 16)
                ch.link(dve.tensor_scalar(T[:, :], idf[:, :], lnc_s, None, ALU.mult))
                ch.link(dve.tensor_scalar(T[0:1, :], T[0:1, :], 0.0, lnc_s[0:1, :], ALU.mult, ALU.subtract))
                ch.link(dve.tensor_copy(T[:, 0:1], lnc_b))
                dve.tensor_copy(nvrep[:, :], nv_c.broadcast_to([128, TT])).then_inc(t_ready, 1)

            def mask_columns():
                dve.wait_ge(ld_m, 16)
                ch.link(dve.tensor_copy(maskf[:, :, :], mask_s[:, :, :]))
                ch.link(dve.tensor_scalar(mbias[:, :, :], maskf[:, :, :], 1.0, MASK_BIAS, ALU.subtract, ALU.mult))
                dve.tensor_scalar(mcol[:, :, :], maskf[:, :, :], 1.0 - MASKED, MASKED, ALU.mult,
                                  ALU.add).then_inc(mask_ready, 1)

            def g_low(s):
                h0 = 8 * (s // 2) + s % 2
                dve.wait_ge(ghi_done, s + 1)
                dve.tensor_tensor(Gl[:, h0:h0 + 7:2, :], S[:, s, :].rearrange("p (t d) -> p t d", d=D),
                                  Gh[:, h0:h0 + 7:2, :], ALU.subtract).then_inc(glo_done, 1)

            def halves():
                dve.wait_ge(xt_copied, 3)
                ch.link(dve.tensor_copy(xTh[:, 0:GTOK], xT[:, 0:GTOK]))
                dve.tensor_tensor(xTl[:, 0:GTOK], xT[:, 0:GTOK], xTh[:, 0:GTOK], ALU.subtract).then_inc(xhl_done, 1)

            dve.wait_ge(ld_x, 16)
            stats(st8, x_s, NT, x8_stats)
            build_t()
            dve.wait_ge(ld_ctx[0], 16)
            stats(st, raw[:, 0], NC, stats_done)
            dve.wait_ge(stats_done, 1)
            ch.link(dve.tensor_tensor(tmp1[:, :], st[:, :, 1], st[:, :, 4], ALU.subtract))
            ch.link(dve.tensor_tensor(tmp2[:, :], tmp1[:, :], tmp1[:, :], ALU.mult))
            ch.link(dve.tensor_scalar(tmp1[:, :], tmp2[:, :], D / 4.0, D * 1e-6, ALU.mult, ALU.add))
            ch.link(dve.tensor_tensor(tmp2[:, :], st[:, :, 2], st[:, :, 5], ALU.add))
            ch.link(dve.tensor_tensor(tmp2[:, :], tmp1[:, :], tmp2[:, :], ALU.add))
            dve.tensor_scalar(tmp1[:, :], tmp2[:, :], 1.0 / D, None, ALU.mult).then_inc(c0_var, 1)
            ch.link(dve.tensor_tensor(mu[:, :], st[:, :, 1], st[:, :, 4], ALU.add))
            ch.link(dve.tensor_scalar(mu[:, :], mu[:, :], 0.5, None, ALU.mult))
            apply_norm(0, xn[:, :, :], x_s[:, :, :], NT, xt_in)
            dve.wait_ge(wt_copied, 4)
            dve.tensor_scalar(WkT[:, :, 0], WkT[:, :, 0], -1.0, nk_c, ALU.mult, ALU.add).then_inc(fold_k, 1)
            dve.tensor_tensor(zf[:, :, :], raw[:, 0], wide12(mu[:, :]), ALU.subtract).then_inc(zc_done, 1)
            mask_columns()
            dve.wait_ge(wt_copied, 6)
            dve.tensor_scalar(WvT[:, :, 0], WvT[:, :, 0], nv_c, None, ALU.subtract).then_inc(fold_v, 1)
            dve.wait_ge(zc_done, 1)
            dve.wait_ge(c0_rs, 1)
            dve.tensor_tensor(zf[:, :, :], zf[:, :, :], wide12(rs[:, :]), ALU.mult).then_inc(z0_done, 1)
            dve.wait_ge(z0_done, 1)
            dve.wait_ge(mask_ready, 1)
            ch.link(dve.tensor_copy(zh[:, 0, 0:HC, 0], mcol[:, 0, 0:HC]))
            ch.link(dve.tensor_copy(zh[:, 0, 0:HC, 1:D], zf[:, 0:HC, 1:D]))
            dve.tensor_tensor(zl[:, 0, 0:HC, 1:D], zf[:, 0:HC, 1:D], zh[:, 0, 0:HC, 1:D],
                              ALU.subtract).then_inc(split1_done, 1)
            for i in range(2):
                g_low(i)
            for i in range(2, 4):
                g_low(i)
            dve.wait_ge(ld_ctx[1], 16)
            stats(st, raw[:, 1], NC, stats_done)

            def residual(step):
                ts = slice(0, GT)
                y = y_s[:, ts, :]
                if step == 0:
                    dve.wait_ge(x8_small, 2)
                    ch.link(dve.tensor_tensor(y, y, wide8(mu8[:, 0:GT], GT), ALU.subtract))
                if step == 1:
                    ch.link(dve.tensor_tensor(y, y, wide8(rs8[:, 0:GT], GT), ALU.mult))
                if step == 2:
                    ch.link(dve.tensor_tensor(y, y, lno_s.unsqueeze(1).broadcast_to([TT, GT, D]), ALU.mult))
                if step == 3:
                    ch.link(dve.tensor_tensor(y, y, lno_b.unsqueeze(1).broadcast_to([TT, GT, D]), ALU.add))
                if step == 4:
                    dve.wait_ge(tanh_done, 1)
                    ch.link(dve.scalar_tensor_tensor(x_s[:, ts, :], y, gates[:, 0:1], x_s[:, ts, :], ALU.mult, ALU.add))
                if step == 5:
                    stats(st8, x_s[:, ts, :], GT, x8_stats)

            def tokens():
                ts = slice(0, GT)
                dve.wait_ge(x8_small, 3)
                ch.link(dve.tensor_tensor(xn[:, ts, :], x_s[:, ts, :], wide8(mu8[:, 0:GT], GT), ALU.subtract))
                dve.tensor_tensor(xn[:, ts, :], xn[:, ts, :], wide8(rs8[:, 0:GT], GT), ALU.mult).then_inc(xt_in, 1)

            def route(g):
                ts = slice(g * GT, (g + 1) * GT)
                scg, eq, oh = sc[:, ts, :], eqm[:, ts, :], oneh[:, ts, :]
                erow_w = erow[:, :].unsqueeze(1).broadcast_to([TT, GT, E])
                dve.wait_ge(sc_ready, g + 1)
                dve.tensor_tensor(scg, X[0:TT, 1, 0:GT * E].rearrange("p (t e) -> p t e", e=E),
                                  br_r.unsqueeze(1).broadcast_to([TT, GT, E]), ALU.add).then_inc(sc_copied, 1)
                dve.wait_ge(sc_copied, g + 1)
                ch.link(dve.reduce_max(scm[:, ts], scg, AX))
                ch.link(dve.tensor_tensor(eq, scg, scm[:, ts].unsqueeze(2).broadcast_to([TT, GT, E]), ALU.is_equal))
                ch.link(dve.tensor_tensor(eq, eq, erow_w, ALU.mult))
                ch.link(dve.tensor_reduce(esel[:, ts], eq, AX, ALU.min))
                ch.link(dve.tensor_tensor(oh, erow_w, esel[:, ts].unsqueeze(2).broadcast_to([TT, GT, E]), ALU.is_equal))
                dve.tensor_scalar(onehs[:, ts, :], oh, 1.0 / W_SCALE, None, ALU.mult).then_inc(oneh_done, 1)

            def sub(b, c):
                k = c % PB
                dve.wait_ge(hi_done, NC * b + c + 1)
                dve.tensor_tensor(Pl[:, k, :].rearrange("p (a r) -> p a r", a=2),
                                  S[0:CK, 2 * (c % 2):2 * (c % 2) + 2, 0:HR],
                                  Ph[:, k, :].rearrange("p (a r) -> p a r", a=2), ALU.subtract).then_inc(lo_done, 1)

            def reciprocals(b, p):
                dve.wait_ge(s7_in, 16 * (b + 1))
                dve.wait_ge(p0_done, b + 1)
                ch.link(dve.tensor_tensor(tot7[:, :], S7[:, :], P07[:, p, :], ALU.add))
                dve.reciprocal(R7[:, :], tot7[:, :]).then_inc(r_done, 1)

            def take_y(b, bank):
                dve.wait_ge(y_ready, b)
                dst = y_s[:, :, :].rearrange("p t d -> p (t d)")
                lo_ = (b - 2) * (D // 2)
                v = dst[:, lo_:lo_ + D] if isinstance(b, int) else dst[:, bass.ds(lo_, D)]
                dve.scalar_tensor_tensor(v, X[0:TT, bank, 0:D], 1.0 / W_SCALE, NVb[:, :], ALU.mult,
                                         ALU.add).then_inc(y_done, 2)

            def queries(n, p, j, banks=X):
                dve.wait_ge(null_done, 2 * n + j + 1)
                dve.scalar_tensor_tensor(ql[:, p, j * HR:(j + 1) * HR], banks[:, j, 0:HR], rowmask[:, 0:1],
                                         qh[:, p, j * HR:(j + 1) * HR], ALU.mult,
                                         ALU.subtract).then_inc(qlo_done, 1)

            def zt_copy(nb, p, j):
                dst, done = ((zTh, zth_copied), (zTl, ztl_copied))[j % 2]
                c0 = HC * CK * (j // 2)
                dve.wait_ge(zt_ready, 4 * nb + j + 1)
                dve.tensor_copy(dst[:, p, c0:c0 + HC * CK].rearrange("p (c k) -> p c k", k=CK),
                                XT[j % 2][:, :, 0:CK]).then_inc(done, 1)

            def a_copy(b, b_ge1):
                dve.wait_ge(pv_done, NC * b + NC)
                if b_ge1:
                    dve.wait_ge(an_done, b)
                dve.tensor_copy(Af[:, :].rearrange("d (a r) -> d a r", a=2), A[:, :, 0:HR]).then_inc(a_copied, 1)

            def context_stats(n, p, ks, ld_value):
                if ks[0] == 0:
                    dve.wait_ge(zc_done, n)
                    dve.wait_ge(ld_ctx[p], ld_value)
                for k in ks:
                    ins = dve.bn_stats(st[:, k, :], raw[:, p, k, :])
                if ks[-1] == NC - 1:
                    ins.then_inc(stats_done, 1)

            def reduce(nb, j):
                blk, t = divmod(j, RT)
                dve.wait_ge(mx_ready, NMX * nb + j + 1)
                dve.reduce_max(mx3[:, t, blk:blk + 1], X[:, j % 2, 0:KB], AX).then_inc(mx_red, 1)

            def body(b, p, f):
                nb, np_ = b + 1, 1 - p
                for c in range(NC):
                    j0 = 3 * (c - 2)
                    maxima = f["prep"] and 2 <= c <= 8
                    if maxima and c == 3:
                        dve.wait_ge(null_in, 16 * (nb + 1))
                        dve.tensor_scalar(null7s[:, :], null7[:, :], SHIFT - 1.0, None, ALU.add).then_inc(ns_done, 1)
                    if maxima:
                        reduce(nb, j0)
                        reduce(nb, j0 + 1)
                    if maxima and c == 8:
                        reduce(nb, j0 + 2)
                    if c == 9 and f["prep"]:
                        dve.wait_ge(mx_red, NMX * (nb + 1))
                        dve.wait_ge(ns_done, nb + 1)
                        ch.link(dve.tensor_reduce(negm[:, :], mx3[:, :, :], AX, ALU.max, negate=True))
                        dve.scalar_tensor_tensor(mneg[:, :], negm[:, :], SHIFT - 2.0, null7s[:, :], ALU.add,
                                                 ALU.min).then_inc(mneg_done, 1)
                        dve.wait_ge(mneg_done, nb + 1)
                        if f["prev"]:
                            dve.wait_ge(p0_done, nb)
                        dve.scalar_tensor_tensor(t7[:, :], mneg[:, :], 1.0, null7[:, :], ALU.add,
                                                 ALU.subtract).then_inc(t7_done, 1)
                    if c == NC - 1 and f["main"] and f["prep"]:
                        a_copy(b, f["tail"])
                    late = c == 10 and not f["y"]
                    if c >= 10 and f["znext"] and not late:
                        queries(b + 2, p, c - 10)
                    if c == 9 and f["load"]:
                        context_stats(b + 3, 1 - p, range(HC), 16 * ((b - p) // 2 + 2 + p) if isinstance(b, int)
                                      else (b - p) * 8 + 32 + 16 * p)
                    zts = f["main"] and f["prep"]
                    if c < 2 and zts:
                        zt_copy(nb, np_, 2 * c)
                        zt_copy(nb, np_, 2 * c + 1)
                    if (f["main"] and c + 2 < NC) or (f["prep"] and c + 2 >= NC):
                        sub(*ahead(b, c))
                    if f["znext"] and late:
                        queries(b + 2, p, c - 10)
                    if maxima and c < 8:
                        reduce(nb, j0 + 2)
                    if c < 2 and zts:
                        if f["znext"]:
                            context_stats(b + 2, p, range(HC + 3 * c, HC + 3 * c + 3), None)
                    if f["group"]:
                        if c == 0:
                            dve.wait_ge(y_done, NT)
                            stats(st8, y_s[:, 0:GT, :], GT, x8_stats)
                        if 2 <= c <= 4:
                            residual(2 * (c - 2))
                            residual(2 * (c - 2) + 1)
                        if c == 7:
                            tokens()
                        if c == 9:
                            halves()
                        if c == 11:
                            route(0)
                    if c == 5 and f["tail"]:
                        reciprocals(b - 1, 1 - p)
                    if c == NC - 1 and f["y"]:
                        take_y(b, 0)

            queries(0, 0, 0, S[:, 2:4, :])
            queries(0, 0, 1, S[:, 2:4, :])
            for b in (-1, 0, 1):
                body(b, b % 2, flags(b))
            n0, PER = ch.n, 1 + 1
            with dve.Fori(2, B - 5, 2) as i:
                ch.base, ch.n = PER * i - 2 * PER + n0, 0
                body(i, 0, STEADY[0])
                assert ch.n == PER
                body(i + 1, 1, STEADY[1])
                assert ch.n == 2 * PER
            ch.base, ch.n = 0, n0 + (B - 6) * PER
            for b in range(B - 4, B):
                body(b, b % 2, flags(b))
            YB = [A[0:TT, 0, 0:D], A[0:TT, 1, 0:D], X[0:TT, 0, 0:D]]

            def gather(n, t):
                k, e = GT * n + t, n % E
                tile = (n // E) * GT + t
                dve.wait_ge(ye_ready, k + 1)
                if e == 0:
                    dve.tensor_scalar(moe[:, tile, :], YB[k % 3], onehs[:, tile, e:e + 1], None,
                                      ALU.mult).then_inc(ye_done, 1)
                else:
                    dve.wait_ge(ye_done, k - GT + 1)
                    dve.scalar_tensor_tensor(moe[:, tile, :], YB[k % 3], onehs[:, tile, e:e + 1], moe[:, tile, :],
                                             ALU.mult, ALU.add).then_inc(ye_done, 1)

            def low(g):
                n, f = divmod(g, FC)
                dve.wait_ge(gh_done, g + 1)
                dve.tensor_tensor(gl[n % 2][:, f, :], S[:, g % 4, 0:GTOK], gh[:, n % 2, f, :],
                                  ALU.subtract).then_inc(gl_done, 1)

            def finish(g):
                ts = slice(g * GT, (g + 1) * GT)
                dve.wait_ge(ye_done, GT * E * (g + 1))
                dve.wait_ge(b2_copied, g + 1)
                dve.tensor_tensor(moe[:, ts, :], moe[:, ts, :], b2s[:, :, :], ALU.add).then_inc(moe_fin, 1)
                dve.wait_ge(moe_fin, g + 1)
                dve.scalar_tensor_tensor(xn[:, ts, :], moe[:, ts, :], gates[:, 1:2], x_s[:, ts, :], ALU.mult,
                                         ALU.add).then_inc(fin_done, 1)

            for g in range(NG * E * FC):
                if g == 2:
                    a_copy(B - 1, True)
                low(g)
                if g >= FC:
                    gather((g - FC) // GT, g % GT)
                if g == 4:
                    reciprocals(B - 1, 1)
                if g == Y_DVE:
                    take_y(B, 1)
                    dve.wait_ge(y_done, B)
                    stats(st8, y_s[:, GT:NT, :], GT, x8_stats)
                if g == X1_DVE:
                    dve.wait_ge(x1_done, 1)
                    stats(st8, x_s[:, GT:NT, :], GT, x8_stats)
                if g == 33:
                    route(1)
                if g == 37:
                    finish(0)
            for t in range(GT):
                gather(NG * E - 1, t)
            finish(1)

        @block.tensor
        def _(pe):
            mm = pe.matmul
            pe.wait_ge(ld_idf, 16)
            pe.wait_ge(ld_wq, 16)
            for s in range(6):
                if s >= 2:
                    pe.wait_ge(wt_copied, s - 1)
                if s == 2:
                    pe.wait_ge(t_ready, 1)
                    pe.wait_ge(ld_wk, 16)
                if s == 4:
                    pe.wait_ge(ld_wv, 16)
                for i in range(4):
                    t = 4 * (s % 2) + i
                    o = X[:, s % 2, i * D:(i + 1) * D]
                    if s < 2:
                        ins = pe.transpose(o, Wq_s[:, t * 128:(t + 1) * 128], idf[:, :])
                    else:
                        w0 = (s // 2 - 1) * INNER + t * 128
                        ins = mm(o, Wkv_s[:, w0:w0 + 128], T[:, :], start=True, stop=True)
                ins.then_inc(wt_ready, 1)
            def head_product(s, i, lhs, rhs, bank):
                h = 8 * (s // 2) + s % 2 + 2 * i
                r0 = DH * (h % 2)
                return mm(bank[:, i * D:(i + 1) * D], lhs[r0:r0 + DH, h // 2, :], rhs[r0:r0 + DH, h // 2, :],
                          start=True, stop=True)

            def transpose_tokens(i, t0, bank):
                pe.wait_ge(xt_in, i + 1)
                for t in range(GT):
                    ins = pe.transpose(bank[:, t * TT:(t + 1) * TT], xn[:, t0 + t, :], idf[0:TT, 0:TT])
                ins.then_inc(xt_ready, 1)

            transpose_tokens(0, 0, A[:, 0])
            transpose_tokens(0, GT, A[:, 1])
            for s in range(4):
                if s == 0:
                    pe.wait_ge(fold_k, 1)
                for i in range(4):
                    ins = head_product(s, i, WqT, WkT, S[:, s, :])
                ins.then_inc(g_ready, 1)

            def value_step(k):
                if k < 16:
                    s, i = divmod(k, 4)
                    if i == 0:
                        pe.wait_ge(*((xt_copied, s + 1) if s < 2 else (m_copied, s - 1)))
                    ins = head_product(s, i, WvT, Wo_s, A[:, s % 2, :])
                    if i == 3:
                        ins.then_inc(m_ready, 1)
                elif k < 16 + NP:
                    t = k - 16
                    if t == 0:
                        pe.wait_ge(m_copied, 3)
                    ins = mm(A[0:TT, 0, 0:D], nvrep[:, :], Wo_s[:, t, :], start=(t == 0), stop=(t == NP - 1))
                    if t == NP - 1:
                        ins.then_inc(nv_ready, 1)
                else:
                    pe.wait_ge(ld_f, 16 * 4)
                    pe.wait_ge(m_copied, 4)
                    pe.transpose(A[:, 1, 0:E * FC], b1_s[:, :], idf[0:E * FC, 0:E * FC]).then_inc(b1_ready, 1)

            def sim(b, c, p):
                if c == 0:
                    pe.wait_ge(slot_done, b + 1)
                    pe.wait_ge(qlo_done, 2 * b + 2)
                    pe.wait_ge(zth_copied, 2 * b + 2)
                    pe.wait_ge(ztl_copied, 2 * b + 2)
                if not (isinstance(b, int) and NC * b + c < 2):
                    pe.wait_ge(lo_done, NC * b + c - 1)
                ks = slice(c * CK, (c + 1) * CK)
                for n, (z, q) in enumerate(((zTh, qh), (zTh, ql), (zTl, qh))):
                    for a in range(2):
                        ins = mm(S[0:CK, 2 * (c % 2) + a, 0:HR], z[:, p, ks], q[:, p, a * HR:(a + 1) * HR],
                                 start=(n == 0), stop=(n == 2))
                ins.then_inc(sim_done, 1)

            def pv(b, c, p, b_ge1, half):
                if c == 0 and half == 0:
                    if b_ge1:
                        pe.wait_ge(a_copied, b)
                    else:
                        pe.wait_ge(m_copied, 5)
                        pe.wait_ge(m_split, 1)
                        pe.wait_ge(b1_copied, 1)
                k, n = c % PB, 0
                if half == 0:
                    pe.wait_ge(hi_done, NC * b + c + 1)
                for z, q, a in ((zh, Ph, 0), (zh, Ph, 1), (zl, Ph, 0), (zl, Ph, 1), (zh, Pl, 0), (zh, Pl, 1)):
                    if n // 3 == half:
                        if n == 4:
                            pe.wait_ge(lo_done, NC * b + c + 1)
                        ins = mm(A[:, a, 0:HR], z[:, p, c, :], q[:, k, a * HR:(a + 1) * HR],
                                 start=(c == 0 and n < 2), stop=(c == NC - 1 and n >= 4))
                    n += 1
                if half == 1:
                    ins.then_inc(pv_done, 1)

            def zt(nb, p, j):
                z = (zh, zl)[j % 2]
                for i in range(HC):
                    ins = pe.transpose(XT[j % 2][:, i, 0:CK], z[:, p, HC * (j // 2) + i, :], idh[0:CK, 0:CK])
                ins.then_inc(zt_ready, 1)

            def queries(n, p, j, n_ge1, banks=X):
                if n_ge1 and j == 0:
                    pe.wait_ge(slot_done, n)
                xh, xl = (v[:, n * NQ:(n + 1) * NQ] if isinstance(n, int) else v[:, bass.ds(n * NQ, NQ)]
                          for v in (xTh, xTl))
                for i in range(H // 2):
                    h = j * (H // 2) + i
                    o = banks[:, j, i * NQ:(i + 1) * NQ]
                    mm(o, Gh[:, h, :], xh, start=True, stop=False)
                    mm(o, Gh[:, h, :], xl, start=False, stop=False)
                    ins = mm(o, Gl[:, h, :], xh, start=False, stop=True)
                ins.then_inc(q_ready, 1)

            def aux(b, p, c, part, f):
                nb, np_ = b + 1, 1 - p
                if c == 0 and part < 2 and f["main"]:
                    pe.wait_ge(qlo_done, 2 * nb + 1 + part)
                    if part == 0:
                        if f["t0y"]:
                            pe.wait_ge(y_done, b - 1)
                        pe.wait_ge(split1_done, nb + 1)
                    zt(nb, np_, part)
                if c == 1 and part < 2 and f["main"]:
                    pe.wait_ge((split2h_done, split2_done)[part], nb + 1)
                    pe.wait_ge((zth_copied, ztl_copied)[part], 2 * nb + 1)
                    zt(nb, np_, 2 + part)
                if 2 <= c <= 8:
                    j = 3 * (c - 2) + part
                    blk, t = divmod(j, RT)
                    if j < 2:
                        pe.wait_ge((zth_copied, ztl_copied)[j], 2 * nb + 2)
                        if not f["main"]:
                            pe.wait_ge(qhi_done, 2)
                    else:
                        pe.wait_ge(mx_red, NMX * nb + j - 1)
                    mm(X[:, j % 2, 0:KB], qh[:, np_, t:R:RT], zTh[:, np_, blk * KB:(blk + 1) * KB],
                       start=True, stop=True).then_inc(mx_ready, 1)
                    if not f["main"] and j % 2:
                        value_step(4 + j // 2)
                if c == 9 and not f["main"] and part == 1:
                    value_step(14)
                    value_step(15)
                if c == 9 and part == 2:
                    pe.wait_ge(mneg_done, nb + 1)
                    for t in range(RT):
                        ins = mm(X[0:1, t // 4, (t % 4) * 128:(t % 4 + 1) * 128], mneg[:, t:t + 1], idh[:, :],
                                 start=True, stop=True)
                    ins.then_inc(mt_ready, 1)
                    if not f["main"]:
                        for k in range(16, 17 + NP):
                            value_step(k)
                if c == 10 and part >= 1 and f["znext"]:
                    queries(b + 2, p, part - 1, True)

            def project(b, bank):
                pe.wait_ge(an_done, b)
                for h in range(H):
                    ah, al = (v[:, h, :, :].rearrange("d u n -> d (u n)") for v in (Anh, Anl))
                    y = X[0:TT, bank, 0:D]
                    mm(y, ah, Mh[:, h, :], start=(h == 0), stop=False)
                    mm(y, ah, Ml[:, h, :], start=False, stop=False)
                    ins = mm(y, al, Mh[:, h, :], start=False, stop=(h == H - 1))
                ins.then_inc(y_ready, 2)

            def body(b, p, f):
                for c in range(NC):
                    scores = f["main"] if c + 2 < NC else f["prep"]
                    if c == 10 and f["main"]:
                        pv(b, c, p, f["tail"], 0)
                        pv(b, c, p, f["tail"], 1)
                    experts = f["group"] and c == NC - 1
                    if experts:
                        route(0)
                        pv(b, c, p, f["tail"], 0)
                        up(0)
                        up(1)
                        pv(b, c, p, f["tail"], 1)
                    if scores:
                        sim(*ahead(b, c), p if c + 2 < NC else 1 - p)
                    for part in range(3):
                        if f["prep"]:
                            aux(b, p, c, part, f)
                        if f["main"] and c != 10 and not experts and part < 2:
                            pv(b, c, p, f["tail"], part)
                    if f["group"] and c == 9:
                        transpose_tokens(1, 0, X[:, 1])
                    if experts:
                        up(2)
                        up(3)
                    if c == NC - 1 and f["y"]:
                        if f["znext"]:
                            pe.wait_ge(qlo_done, 2 * b + 5)
                        else:
                            pe.wait_ge(slot_done, b + 2)
                        project(b, 0)

            def route(g):
                pe.wait_ge(xt_copied, g + 3)
                for t in range(GT):
                    tile = g * GT + t
                    ins = mm(X[0:TT, 1, t * E:(t + 1) * E], xT[:, tile * TT:(tile + 1) * TT], wr_s[:, :],
                             start=True, stop=True)
                ins.then_inc(sc_ready, 1)

            def one_hot(g):
                pe.wait_ge(oneh_done, g + 1)
                for t in range(GT):
                    ins = pe.transpose(X[0:E, 1, t * TT:(t + 1) * TT], oneh[:, g * GT + t, :], idf[0:TT, 0:TT])
                ins.then_inc(ohT_ready, 1)

            def bias2(g):
                pe.wait_ge(ohT_copied, g + 1)
                for t in range(GT):
                    ins = mm(X[0:TT, 1, t * D:(t + 1) * D], onehT[:, g * GT + t, :], b2_s[:, :],
                             start=True, stop=True)
                ins.then_inc(b2_ready, 1)

            def up(g):
                n, f = divmod(g, FC)
                e = n % E
                if g < 4:
                    pe.wait_ge(lo_done, NC * B - 1 + g // 2)
                else:
                    pe.wait_ge(gl_done, g - 3)
                if f == 0:
                    pe.wait_ge(wsplit, e + 1)
                    pe.wait_ge(xhl_done, 3 + n // E)
                xs = slice((n // E) * GTOK, (n // E + 1) * GTOK)
                for i, (w, xx) in enumerate(((wh, xTh), (wh, xTl), (wl, xTh))):
                    ins = mm(S[:, g % 4, 0:GTOK], w[:, e, 0, f * 128:(f + 1) * 128], xx[:, xs],
                             start=(i == 0), stop=(i == 2))
                ins.then_inc(h_ready, 1)

            YB = [A[0:TT, 0, 0:D], A[0:TT, 1, 0:D], X[0:TT, 0, 0:D]]

            def down(n, t):
                k, e, p = GT * n + t, n % E, n % 2
                if k == 0:
                    pe.wait_ge(a_copied, B)
                if k >= 3:
                    pe.wait_ge(ye_done, k - 2)
                i = 0
                for f in range(FC):
                    if t == 0:
                        pe.wait_ge(gl_done, FC * n + f + 1)
                    for gg, w in ((gh[:, p], wh), (gh[:, p], wl), (gl[p], wh)):
                        ins = mm(YB[k % 3], gg[:, f, t * TT:(t + 1) * TT], w[:, e, 1, f * D:(f + 1) * D],
                                 start=(i == 0), stop=(i == 3 * FC - 1))
                        i += 1
                ins.then_inc(ye_ready, 1)

            pe.wait_ge(fold_v, 1)
            pe.wait_ge(ld_wo, 16)
            for k in range(4):
                value_step(k)
            pe.wait_ge(ld_idh, 16)
            pe.wait_ge(split1_done, 1)
            pe.wait_ge(wt_copied, 6)
            zt(0, 0, 0)
            zt(0, 0, 1)
            pe.wait_ge(split2_done, 1)
            pe.wait_ge(zth_copied, 1)
            zt(0, 0, 2)
            pe.wait_ge(ztl_copied, 1)
            zt(0, 0, 3)
            pe.wait_ge(xhl_done, 2)
            pe.wait_ge(glo_done, 4)
            queries(0, 0, 0, False, S[:, 2:4, :])
            queries(0, 0, 1, False, S[:, 2:4, :])

            iterate(pe, body, B - 2)

            LEAD = FC + 1
            for g in range(4, LEAD):
                up(g)
            one_hot(0)
            for k in range(NG * E * GT):
                if k + LEAD < NG * E * FC:
                    up(k + LEAD)
                down(k // GT, k % GT)
                if k == 2:
                    bias2(0)
                if k == Y_PE:
                    pe.wait_ge(b2_copied, 1)
                    project(B, 1)
                if k == XT_PE:
                    pe.wait_ge(y_done, B)
                    transpose_tokens(2, GT, X[:, 1])
                if k == 28:
                    route(1)
                if k == 33:
                    one_hot(1)
                if k == 40:
                    bias2(1)


_INS = ['Wq', 'Wkv', 'Wo', 'wr', 'w1', 'b1', 'w2', 'b2']


def kernel(**inputs):
    import numpy as _np
    import concourse.bacc as _bacc
    from concourse import mybir as _mybir
    from concourse.bass_utils import run_bass_kernel_spmd as _run

    nc = _bacc.Bacc("TRN2", target_bir_lowering=False, num_devices=1)
    arrays, args = {}, []

    def give(name, a):
        arrays[name] = a
        args.append(nc.dram_tensor(name, a.shape, _mybir.dt.from_np(a.dtype), kind="ExternalInput").ap())

    give("x_dram", _np.ascontiguousarray(inputs["x"]))
    give("ctx_dram", _np.ascontiguousarray(inputs["ctx_1024"]))
    give("mask_dram", _np.ascontiguousarray(inputs["mask_BxS2_bf1"]).view(_np.uint8))
    nk, nv = _np.asarray(inputs["L0_xattn_null_kv"])
    give("cols_dram", _np.stack([inputs["L0_xattn_lnc_s"], inputs["L0_xattn_lnc_b"], inputs["L0_xattn_ln1_s"],
                                 inputs["L0_xattn_ln1_b"], _np.tile(nk, 2), _np.tile(nv, 2)], axis=1))
    give("rows_dram", _np.concatenate([inputs["L0_xattn_lno_s"], inputs["L0_xattn_lno_b"], inputs["L0_ffn_br"],
                                       inputs["g_xattn"], inputs["g_ffn"]])[None, :])
    for name in _INS:
        full = ("L0_xattn_" if name[0] == "W" else "L0_ffn_") + name
        give(f"in_{name}_dram", _np.ascontiguousarray(inputs[full]))
    give("ident_f32_dram", _np.eye(128, dtype=_np.float32))
    give("ident_f16_dram", _np.eye(128, dtype=_np.float16))
    args.append(nc.dram_tensor("out_dram", (16, 56, 128), _mybir.dt.float32, kind="ExternalOutput").ap())
    gated_cross_attention_moe_kernel(nc, *args)
    r = _run(nc, [arrays], core_ids=[0])
    return r.results[0]["out_dram"]
```
